# Optimizing a Trainium2 kernel written in Bass

```python
import numpy as np
import jax
import jax.numpy as jnp

def _softmax(x, axis=-1):
    return jax.nn.softmax(x, axis=axis)

def _gelu(x):
    return jax.nn.gelu(x, approximate=True)

def _silu(x):
    return jax.nn.silu(x)

def _sigmoid(x):
    return jax.nn.sigmoid(x)

def _layernorm(x, axis=-1, eps=1e-05):
    m = jnp.mean(x, axis=axis, keepdims=True)
    v = jnp.var(x, axis=axis, keepdims=True)
    return (x - m) / jnp.sqrt(v + eps)

def _scatter_add(tgt, idx, src, axis=0):
    return tgt.at[idx].add(src)

def _segment_sum(src, seg, n):
    return jax.ops.segment_sum(src, seg, n)
kernel_name = 'mk_vit_tower_d1_tok_img768_r4_e944db'

def setup_inputs(seed: int=0):
    np.random.seed(seed)
    _w = jnp.asarray

    def _rec_inputs():
        import jax
        import jax.numpy as jnp
        _rk = jax.random.key(seed)
        x = -0.000125008 + 0.999885 * jax.random.normal(jax.random.fold_in(_rk, 1), (64, 4, 96, 96), jnp.float32)
        return x
    x = _rec_inputs()

    def _L0_tok_setup():
        import jax, jax.numpy as jnp
        import numpy as np
        P = 32
        C = 4
        PATCH_DIM = C * P * P
        HIDDEN = 192
        EPS = 1e-05

        def _layernorm(x, gamma, beta):
            mu = jnp.mean(x, axis=-1, keepdims=True)
            var = jnp.mean(jnp.square(x - mu), axis=-1, keepdims=True)
            return (x - mu) * jax.lax.rsqrt(var + EPS) * gamma + beta
        key = jax.random.key(seed)
        ks = jax.random.split(key, 6)
        B, H, W = (32, 128, 128)
        x = jax.random.normal(ks[0], (B, C, H, W), dtype=jnp.float32)
        ln1_g = jnp.ones((PATCH_DIM,), jnp.float32)
        ln1_b = jnp.zeros((PATCH_DIM,), jnp.float32)
        W_proj = jax.random.normal(ks[1], (PATCH_DIM, HIDDEN), jnp.float32) / np.sqrt(PATCH_DIM)
        b_proj = jnp.zeros((HIDDEN,), jnp.float32)
        ln2_g = jnp.ones((HIDDEN,), jnp.float32)
        ln2_b = jnp.zeros((HIDDEN,), jnp.float32)
        return {'x': x, 'ln1_g': ln1_g, 'ln1_b': ln1_b, 'W_proj': W_proj, 'b_proj': b_proj, 'ln2_g': ln2_g, 'ln2_b': ln2_b}
    _L0_tok_all = _L0_tok_setup()
    _L0_tok_in = {k: v for k, v in _L0_tok_all.items() if k in ('ln1_g', 'ln1_b', 'W_proj', 'b_proj', 'ln2_g', 'ln2_b')}
    del _L0_tok_all

    def _L0_attn_setup():
        import jax, jax.numpy as jnp
        import numpy as np
        import math
        EMBED_DIM = 192
        NUM_HEADS = 12
        N_QUBITS = 96
        D_K = N_QUBITS // NUM_HEADS
        key = jax.random.key(seed)
        k1, k2, k3 = jax.random.split(key, 3)
        x = jax.random.normal(k1, (8, 256, EMBED_DIM), dtype=jnp.float32)
        theta = jax.random.uniform(k2, (N_QUBITS,), dtype=jnp.float32, minval=-math.pi, maxval=math.pi)
        W_combine = jax.random.normal(k3, (EMBED_DIM, N_QUBITS), dtype=jnp.float32) / math.sqrt(N_QUBITS)
        return {'x': x, 'theta': theta, 'W_combine': W_combine}
    _L0_attn_all = _L0_attn_setup()
    _L0_attn_in = {k: v for k, v in _L0_attn_all.items() if k in ('theta', 'W_combine')}
    del _L0_attn_all

    def _L0_ffn_setup():
        import jax, jax.numpy as jnp
        import numpy as np
        B, T, D, E, K = (4, 512, 192, 8, 2)
        H = 4 * D
        key = jax.random.key(seed)
        k0, k1, k2, k3, k4 = jax.random.split(key, 5)
        s = 0.02
        return {'x': jax.random.normal(k0, (B, T, D), jnp.float32), 'router_w': jax.random.uniform(k1, (E, D), jnp.float32, -s * 0.1, s * 0.1), 'Wg': jax.random.uniform(k2, (E, H, D), jnp.float32, -s * 0.4, s * 0.4), 'Wu': jax.random.uniform(k3, (E, H, D), jnp.float32, -s * 0.4, s * 0.4), 'Wd': jax.random.normal(k4, (E, D, H), jnp.float32) * 0.01}
    _L0_ffn_all = _L0_ffn_setup()
    _L0_ffn_in = {k: v for k, v in _L0_ffn_all.items() if k in ('router_w', 'Wg', 'Wu', 'Wd')}
    del _L0_ffn_all
    return {'x': x, 'L0_tok_ln1_g': _L0_tok_in['ln1_g'], 'L0_tok_ln1_b': _L0_tok_in['ln1_b'], 'L0_tok_W_proj': _L0_tok_in['W_proj'], 'L0_tok_b_proj': _L0_tok_in['b_proj'], 'L0_tok_ln2_g': _L0_tok_in['ln2_g'], 'L0_tok_ln2_b': _L0_tok_in['ln2_b'], 'L0_attn_theta': _L0_attn_in['theta'], 'L0_attn_W_combine': _L0_attn_in['W_combine'], 'L0_ffn_router_w': _L0_ffn_in['router_w'], 'L0_ffn_Wg': _L0_ffn_in['Wg'], 'L0_ffn_Wu': _L0_ffn_in['Wu'], 'L0_ffn_Wd': _L0_ffn_in['Wd']}

def reference(x, L0_tok_ln1_g, L0_tok_ln1_b, L0_tok_W_proj, L0_tok_b_proj, L0_tok_ln2_g, L0_tok_ln2_b, L0_attn_theta, L0_attn_W_combine, L0_ffn_router_w, L0_ffn_Wg, L0_ffn_Wu, L0_ffn_Wd):
    import jax
    import jax.numpy as jnp

    def _L0_tok_ref(x, ln1_g, ln1_b, W_proj, b_proj, ln2_g, ln2_b):
        import jax, jax.numpy as jnp
        import numpy as np
        P = 32
        C = 4
        PATCH_DIM = C * P * P
        HIDDEN = 192
        EPS = 1e-05

        def _layernorm(x, gamma, beta):
            mu = jnp.mean(x, axis=-1, keepdims=True)
            var = jnp.mean(jnp.square(x - mu), axis=-1, keepdims=True)
            return (x - mu) * jax.lax.rsqrt(var + EPS) * gamma + beta
        B, c, H, W = x.shape
        h, w = (H // P, W // P)
        patches = x.reshape(B, c, h, P, w, P)
        patches = patches.transpose(0, 2, 4, 3, 5, 1)
        patches = patches.reshape(B, h * w, P * P * c)
        y = _layernorm(patches, ln1_g, ln1_b)
        y = jnp.einsum('bnd,dk->bnk', y, W_proj) + b_proj
        y = _layernorm(y, ln2_g, ln2_b)
        return y

    def _L0_attn_ref(x, theta, W_combine):
        import jax, jax.numpy as jnp
        import numpy as np
        import math
        EMBED_DIM = 192
        NUM_HEADS = 12
        N_QUBITS = 96
        D_K = N_QUBITS // NUM_HEADS
        B, S, _ = x.shape
        xs = x[..., :N_QUBITS]
        q_vecs = jnp.cos(xs) * jnp.cos(theta)
        q = q_vecs.reshape(B, S, NUM_HEADS, D_K).transpose(0, 2, 1, 3)
        scores = jnp.einsum('bhsd,bhtd->bhst', q, q) / math.sqrt(D_K)
        probs = jax.nn.softmax(scores, axis=-1)
        attn = jnp.einsum('bhst,bhtd->bhsd', probs, q)
        attn = attn.transpose(0, 2, 1, 3).reshape(B, S, N_QUBITS)
        return attn @ W_combine.T

    def _L0_ffn_ref(x, router_w, Wg, Wu, Wd):
        import jax, jax.numpy as jnp
        import numpy as np
        B, T, D, E, K = (4, 512, 192, 8, 2)
        H = 4 * D
        Bv, Tv, Dv = x.shape
        N = Bv * Tv
        xf = x.reshape(N, Dv)
        logits = (xf @ router_w.T).astype(jnp.float32)
        top_logits, top_idx = jax.lax.top_k(logits, K)
        top_w = jax.nn.softmax(top_logits, axis=-1).astype(x.dtype)
        out = jnp.zeros_like(xf)
        for e in range(E):
            w_e = jnp.sum(top_w * (top_idx == e), axis=-1)
            h = jax.nn.silu(xf @ Wg[e].T) * (xf @ Wu[e].T)
            out = out + h @ Wd[e].T * w_e[:, None]
        return out.reshape(Bv, Tv, Dv)
    h = _L0_tok_ref(x, L0_tok_ln1_g, L0_tok_ln1_b, L0_tok_W_proj, L0_tok_b_proj, L0_tok_ln2_g, L0_tok_ln2_b)
    h = h + _L0_attn_ref(_layernorm(h, axis=-1), L0_attn_theta, L0_attn_W_combine)
    h = h + _L0_ffn_ref(_layernorm(h, axis=-1), L0_ffn_router_w, L0_ffn_Wg, L0_ffn_Wu, L0_ffn_Wd)
    return h

_drawn_inputs = setup_inputs


def setup_inputs(seed=0):
    import zlib

    import numpy as np

    out = dict(_drawn_inputs(seed))
    spreads = {'L0_tok_ln1_g': (1.0, 0.2),
     'L0_tok_ln1_b': (0.0, 0.1),
     'L0_tok_b_proj': (0.0, 0.1),
     'L0_tok_ln2_g': (1.0, 0.2),
     'L0_tok_ln2_b': (0.0, 0.1)}
    factors = {'L0_ffn_router_w': 8.0, 'L0_ffn_Wg': 8.0, 'L0_ffn_Wu': 8.0, 'L0_ffn_Wd': 8.0}
    for name, (base, spread) in spreads.items():
        noise = np.random.default_rng([zlib.crc32(name.encode()), seed]).standard_normal(out[name].shape)
        drawn = base * np.exp(spread * noise) if base else spread * noise
        out[name] = jnp.asarray(drawn.astype(out[name].dtype))
    for name, factor in factors.items():
        out[name] = (out[name] * factor).astype(out[name].dtype)
    return out
```

```python
import math
from contextlib import ExitStack

import concourse.bass as bass
from concourse import mybir


def vit_tower(nc, x, ln1_g, ln1_b, w_proj, b_proj, ln2_g, ln2_b, theta, w_comb, router,
              w_k1, w_k2, w_down, out, slot_x, slot_y):
    f32 = mybir.dt.float32
    i32 = mybir.dt.int32
    u32 = mybir.dt.uint32
    ALU = mybir.AluOpType
    ACT = mybir.ActivationFunctionType
    AX = mybir.AxisListType.X

    TILES, P, KT, TOKP = x.shape
    TOK = TOKP - 1
    D = w_proj.shape[1]
    D2 = D - P
    KD = KT * P
    SEQ = 9
    IMGS = TOK // SEQ
    NTOK = out.shape[0]
    LAST = NTOK - (TILES - 1) * TOK
    Q = theta.shape[0]
    HEADS = 12
    DK = Q // HEADS
    E = w_k1.shape[0]
    HID = w_k1.shape[2] // 2
    BLK = 256
    STEPS = HID // BLK
    HT = BLK // P
    CHUNK = P
    CHUNKS = (2 * NTOK + E * (CHUNK - 1)) // CHUNK
    EPS = 1e-5
    MAGIC = 1.5 * 2.0 ** 23
    TWO_PI_A = 6.28125
    TWO_PI_B = 2 * math.pi - TWO_PI_A
    RSQRT_SEED = float(0x5F3759DF)
    EW = 2 * 2 * HID + (HID // P) * D
    EARLY = 3

    def spread(ap, dim, n):
        shape = list(ap.shape)
        shape[dim] = n
        return ap.broadcast_to(shape)

    ctx = ExitStack()
    with ctx:
        def sb(name, shape, dt=f32):
            return ctx.enter_context(nc.sbuf_tensor(name, shape, dt))

        def sem(name):
            return ctx.enter_context(nc.semaphore(name))

        experts = sb("experts", [P, E, EW])
        flat = experts[:, :, :].rearrange("p e w -> p (e w)")
        at = EARLY * EW
        wraw = flat[:, at:at + KT * D].rearrange("p (k d) -> p k d", k=KT)
        at += KT * D
        gw = flat[:, at:at + KT * (D + 1)].rearrange("p (k d) -> p k d", k=KT)
        at += KT * (D + 1)
        xbuf = flat[:, at:at + 2 * KT * TOKP].rearrange("p (b k t) -> p b k t", b=2, k=KT)
        at += 2 * KT * TOKP
        assert at <= E * EW
        sq = sb("sq", [P, 2, KT // 4, TOKP])
        ssq = sb("ssq", [P, 2, TOKP])
        gcol = sb("gcol", [P, KT])
        bcol = sb("bcol", [P, KT])
        ones = sb("ones", [P, P])
        identi = sb("identi", [P, P], i32)
        ident = sb("ident", [P, P])
        seli = sb("seli", [P, SEQ, IMGS, SEQ], i32)
        sel = sb("sel", [P, SEQ, TOK])
        before = sb("before", [P, P])
        e_iota_i = sb("e_iota_i", [P, E], i32)
        e_iota = sb("e_iota", [P, E])
        c_iota_i = sb("c_iota_i", [P, CHUNKS, E], i32)
        c_iota = sb("c_iota", [P, CHUNKS, E])
        validi = sb("validi", [P, TILES], i32)
        valid = sb("valid", [P, TILES])
        theta_b = sb("theta_b", [P, Q])
        ln2g_b = sb("ln2g_b", [P, D])
        ln2b_b = sb("ln2b_b", [P, D])
        bproj_b = sb("bproj_b", [P, D])
        wcomb = sb("wcomb", [Q, D])
        rt1 = sb("rt1", [P, E])
        rt2 = sb("rt2", [D2, E])
        halfpi = sb("halfpi", [P, 1])
        ctheta = sb("ctheta", [P, Q])
        c1 = sb("c1", [P, D])
        c2 = sb("c2", [P, D])
        crow = sb("crow", [1, 2, D])
        small = sb("small", [P, 16])
        bns = sb("bns", [P, 6])
        mv = sb("mv", [P, 2])
        rs = sb("rs", [P, 4])
        rsi = sb("rsi", [P, 1], i32)
        y0 = sb("y0", [P, D])
        y1 = sb("y1", [P, D])
        h0 = sb("h0", [P, D])
        ang = sb("ang", [P, 3, Q])
        absr = sb("absr", [P, Q])
        cosx = sb("cosx", [P, Q])
        q = sb("q", [P, Q])
        k9 = sb("k9", [P, SEQ, Q])
        prod = sb("prod", [P, SEQ * Q])
        scores = sb("scores", [P, HEADS * SEQ])
        probs = sb("probs", [P, HEADS * SEQ])
        den = sb("den", [P, 2, HEADS])
        mix = sb("mix", [P, Q])
        o = sb("o", [P, Q])
        oT = sb("oT", [Q, TOK])
        h1 = sb("h1", [P, TILES, D])
        xn = sb("xn", [P, TILES, D])
        xnT = sb("xnT", [P, 2, TOK])
        top = sb("top", [P, TILES, 8])
        logit = sb("logit", [P, 8])
        topi = sb("topi", [P, TILES, 8], u32)
        topf = sb("topf", [P, TILES, 8])
        gap = sb("gap", [P, TILES])
        gexp = sb("gexp", [P, TILES])
        wsel = sb("wsel", [P, 3, TILES])
        hot = sb("hot", [P, 2, TILES, E])
        either = sb("either", [P, TILES, E])
        totals = sb("totals", [P, TILES, E])
        place = sb("place", [P, TILES, E])
        cum = sb("cum", [P, TILES + 1, E])
        nch = sb("nch", [P, 4, E])
        base = sb("base", [P, E])
        posm = sb("posm", [P, 2, TILES, E])
        posf = sb("posf", [P, 2, TILES])
        posi = sb("posi", [P, 2, TILES], u32)
        cmp = sb("cmp", [P, CHUNKS, E])
        cexp = sb("cexp", [P, CHUNKS])
        cexpi = sb("cexpi", [P, 1, CHUNKS], i32)
        xc = sb("xc", [P, 2, D])
        xcT = sb("xcT", [P, 2, 2, CHUNK])
        act = sb("act", [P, 2, BLK])
        hid = sb("hid", [P, 2, BLK])
        hidT = sb("hidT", [P, 2, HT, CHUNK])
        yc = sb("yc", [P, 2, D])
        got = sb("got", [P, 2, TILES, D])
        res = sb("res", [P, TILES, D])

        BANK = 512
        ps = ctx.enter_context(nc.psum_tensor("ps", [P, 8 * BANK], f32))

        def bank(b, n=BANK, rows=P):
            return ps[0:rows, b * BANK:b * BANK + n]

        x_in = [sem("x_in0"), sem("x_in1")]
        w_in = sem("w_in")
        gb_in = sem("gb_in")
        consts_in = sem("consts_in")
        exp_in = [sem(f"exp_in{e}") for e in range(E)]
        experts_ready = sem("experts_ready")
        zero_out = sem("zero_out")
        pool_consts = sem("pool_consts")
        vec_consts = sem("vec_consts")
        ones_ready = sem("ones_ready")
        gw_ready = sem("gw_ready")
        c_rows = sem("c_rows")
        crow_ready = sem("crow_ready")
        c_bcast = sem("c_bcast")
        sq_ready = sem("sq_ready")
        sq_used = sem("sq_used")
        ssq_ready = sem("ssq_ready")
        ssq_done = sem("ssq_done")
        tok_done = sem("tok_done")
        ln1_read = sem("ln1_read")
        abs_ready = sem("abs_ready")
        cos_ready = sem("cos_ready")
        q_ready = sem("q_ready")
        k9_done = sem("k9_done")
        k9_ready = sem("k9_ready")
        scores_ready = sem("scores_ready")
        probs_ready = sem("probs_ready")
        o_ready = sem("o_ready")
        oT_done = sem("oT_done")
        oT_ready = sem("oT_ready")
        proj_done = sem("proj_done")
        xn_ready = sem("xn_ready")
        xnT_done = sem("xnT_done")
        xnT_ready = sem("xnT_ready")
        logits_done = sem("logits_done")
        logits_read = sem("logits_read")
        gap_ready = sem("gap_ready")
        gexp_ready = sem("gexp_ready")
        either_ready = sem("either_ready")
        ranks_done = sem("ranks_done")
        pos_ready = sem("pos_ready")
        cexp_ready = sem("cexp_ready")
        scattered = sem("scattered")
        xc_in = [sem("xc_in0"), sem("xc_in1")]
        xcT_done = sem("xcT_done")
        xcT_ready = sem("xcT_ready")
        gu_done = sem("gu_done")
        act_ready = sem("act_ready")
        hid_ready = sem("hid_ready")
        hidT_done = sem("hidT_done")
        hidT_ready = sem("hidT_ready")
        down_done = sem("down_done")
        y_ready = sem("y_ready")
        y_out = [sem("y_out0"), sem("y_out1")]
        gathered = sem("gathered")
        res_ready = sem("res_ready")
        out_done = sem("out_done")
        vchain = sem("vchain")
        pchain = sem("pchain")

        GS = KT // 4
        N_CONSTS = 7 * 16

        def load_expert(eng, e):
            w = 2 * HID
            eng.dma_start(experts[:, e, 0:w], w_k1[e]).then_inc(exp_in[e], 16)
            eng.dma_start(experts[0:D2, e, w:2 * w], w_k2[e]).then_inc(exp_in[e], 16)
            eng.dma_start(experts[:, e, 2 * w:EW], w_down[e]).then_inc(exp_in[e], 16)

        block = ctx.enter_context(nc.Block())

        @block.sync
        def _(sp):
            def load_x(t):
                sp.dma_start(xbuf[:, t % 2], x[t]).then_inc(x_in[t % 2], 16)

            sp.dma_start(gcol[:, :], ln1_g).then_inc(gb_in, 16)
            sp.dma_start(bcol[:, :], ln1_b).then_inc(gb_in, 16)
            sp.dma_start(wraw, w_proj.rearrange("(p k) d -> p k d", p=P)).then_inc(w_in, 16)
            load_x(0)
            load_x(1)
            for dst, src in ((theta_b, theta), (ln2g_b, ln2_g), (ln2b_b, ln2_b), (bproj_b, b_proj)):
                sp.dma_start(dst[:, :], spread(src.rearrange("(o n) -> o n", o=1), 0, P)).then_inc(consts_in, 16)
            sp.dma_start(wcomb[:, :], w_comb).then_inc(consts_in, 16)
            sp.dma_start(rt1[:, :], router[0:P, :]).then_inc(consts_in, 16)
            sp.dma_start(rt2[:, :], router[P:D, :]).then_inc(consts_in, 16)
            for t in range(2, TILES):
                sp.wait_ge(tok_done, t - 1)
                sp.wait_ge(sq_ready, 4 * (t - 1))
                load_x(t)
            for e in range(EARLY):
                load_expert(sp, e)
            sp.wait_ge(tok_done, TILES)
            sp.wait_ge(sq_ready, 4 * TILES)
            for e in range(EARLY, E):
                load_expert(sp, e)
            sp.wait_ge(scattered, 16 * 2 * TILES)

            def load_chunk(c, b):
                sp.dma_start(xc[:, b, :], slot_x[bass.ts(c, CHUNK), :]).then_inc(xc_in[b], 16)

            def store_chunk(c, b, n):
                sp.wait_ge(y_ready, n)
                sp.dma_start(slot_y[bass.ts(c, CHUNK), :], yc[:, b, :]).then_inc(y_out[b], 16)

            load_chunk(0, 0)
            load_chunk(1, 1)
            with sp.Fori(0, CHUNKS // 2 - 1) as i:
                for b in range(2):
                    sp.wait_ge(xcT_done, 2 * i + (b + 1))
                    load_chunk(2 * i + (b + 2), b)
                    store_chunk(2 * i + b, b, 2 * i + (b + 1))
            for b in range(2):
                store_chunk(CHUNKS - 2 + b, b, CHUNKS - 1 + b)
            flat_out = out
            for t in range(TILES):
                rows = TOK if t < TILES - 1 else LAST
                sp.wait_ge(res_ready, t + 1)
                sp.dma_start(flat_out[t * TOK:t * TOK + rows, :], res[0:rows, t, :]).then_inc(out_done, 16)
            sp.wait_ge(out_done, 16 * TILES)

        @block.gpsimd
        def _(pool):
            steps = [0]

            def link(ins):
                steps[0] += 1
                ins.then_inc(pchain, 1)
                pool.wait_ge(pchain, steps[0])

            nc.gpsimd.memset(ones[:, :], 1.0).then_inc(ones_ready, 1)
            nc.gpsimd.memset(halfpi[:, :], math.pi / 2)
            nc.gpsimd.iota(identi[:, :], pattern=[[-1, P]], base=0, channel_multiplier=1)
            nc.gpsimd.iota(seli[:, :, :, :], pattern=[[-1, SEQ], [-SEQ, IMGS], [0, SEQ]], base=0,
                           channel_multiplier=1)
            nc.gpsimd.iota(e_iota_i[:, :], pattern=[[1, E]], base=0, channel_multiplier=0)
            nc.gpsimd.iota(c_iota_i[:, :, :], pattern=[[1, CHUNKS], [0, E]], base=0, channel_multiplier=0)
            link(nc.gpsimd.iota(validi[:, :], pattern=[[TOK, TILES]], base=0, channel_multiplier=1))
            nc.gpsimd.memset(y0[:, :], 0.0).then_inc(pool_consts, 1)
            pool.wait_ge(pool_consts, 1)
            for c in range(CHUNKS):
                pool.dma_start(slot_x[c * CHUNK:(c + 1) * CHUNK, :], y0[:, :]).then_inc(zero_out, 16)
            for t in range(TILES):
                if t >= 2:
                    pool.wait_ge(ssq_done, t - 1)
                for g in range(4):
                    n = 4 * t + g
                    pool.wait_ge(sq_ready, n + 1)
                    s = sq[:, n % 2]
                    link(nc.gpsimd.tensor_tensor(s[:, 0:GS // 2], s[:, 0:GS // 2], s[:, GS // 2:GS], ALU.add))
                    link(nc.gpsimd.tensor_tensor(s[:, 0:GS // 4], s[:, 0:GS // 4], s[:, GS // 4:GS // 2], ALU.add))
                    ins = nc.gpsimd.tensor_tensor(s[:, 0], s[:, 0], s[:, 1], ALU.add)
                    if g == 0:
                        link(ins)
                        last = nc.gpsimd.tensor_copy(ssq[:, t % 2, :], s[:, 0])
                    else:
                        link(ins)
                        last = nc.gpsimd.tensor_tensor(ssq[:, t % 2, :], ssq[:, t % 2, :], s[:, 0], ALU.add)
                    last.then_inc(sq_used, 1)
                    pool.wait_ge(sq_used, n + 1)
                nc.gpsimd.drain().then_inc(ssq_ready, 1)
            pool.wait_ge(zero_out, 16 * CHUNKS)
            pool.wait_ge(pos_ready, 1)
            for t in range(TILES):
                rows = TOK if t < TILES - 1 else LAST
                for k in range(2):
                    pool.indirect_dma_start(
                        out=slot_x, out_offset=bass.IndirectOffsetOnAxis(ap=posi[0:rows, k, t:t + 1], axis=0),
                        in_=xn[0:rows, t, :], in_offset=None).then_inc(scattered, 16)
            for e in range(E):
                pool.wait_ge(exp_in[e], 48)
                pool.sem_inc(experts_ready, 1)
            pool.wait_ge(y_out[0], 16 * (CHUNKS // 2))
            pool.wait_ge(y_out[1], 16 * (CHUNKS // 2))
            for t in range(TILES):
                rows = TOK if t < TILES - 1 else LAST
                for k in range(2):
                    pool.indirect_dma_start(
                        out=got[0:rows, k, t, :], out_offset=None, in_=slot_y,
                        in_offset=bass.IndirectOffsetOnAxis(ap=posi[0:rows, k, t:t + 1], axis=0)).then_inc(gathered, 16)

        @block.scalar
        def _(sc):
            def cosine(n, dst):
                sc.wait_ge(abs_ready, n + 1)
                nc.scalar.activation(dst, absr[0:TOK, :], ACT.Sin, bias=halfpi[0:TOK, 0:1], scale=-1.0).then_inc(cos_ready, 1)

            sc.wait_ge(pool_consts, 1)
            cosine(0, ctheta[0:TOK, :])
            sc.wait_ge(c_rows, 2)
            nc.scalar.copy(crow[:, :, :], bank(7, 2 * D, 1).rearrange("p (a d) -> p a d", a=2)).then_inc(crow_ready, 1)

            def squares(t):
                sc.wait_ge(x_in[t % 2], 16 * (t // 2 + 1))
                for g in range(4):
                    n = 4 * t + g
                    if n >= 2:
                        sc.wait_ge(sq_used, n - 1)
                    nc.scalar.activation(sq[:, n % 2], xbuf[:, t % 2, g * GS:(g + 1) * GS, :],
                                         ACT.Square).then_inc(sq_ready, 1)

            squares(0)
            for t in range(TILES):
                if t + 1 < TILES:
                    squares(t + 1)
                cosine(t + 1, cosx[0:TOK, :])
                sc.wait_ge(k9_done, t + 1)
                nc.scalar.copy(k9[0:TOK, 0:5], bank(2, 5 * Q, TOK).rearrange("p (j f) -> p j f", f=Q))
                nc.scalar.copy(k9[0:TOK, 5:SEQ], bank(3, 4 * Q, TOK).rearrange("p (j f) -> p j f", f=Q)).then_inc(k9_ready, 1)
                sc.wait_ge(scores_ready, t + 1)
                nc.scalar.activation(probs[0:TOK, :], scores[0:TOK, :], ACT.Exp, scale=DK ** -0.5).then_inc(probs_ready, 1)
                sc.wait_ge(oT_done, t + 1)
                nc.scalar.copy(oT[:, :], bank(4, TOK, Q)).then_inc(oT_ready, 1)
                sc.wait_ge(xnT_done, t + 1)
                nc.scalar.copy(xnT[:, 0, :], bank(4, TOK))
                nc.scalar.copy(xnT[0:D2, 1, :], ps[0:D2, 4 * BANK + TOK:4 * BANK + 2 * TOK]).then_inc(xnT_ready, 1)
            sc.wait_ge(gap_ready, 1)
            nc.scalar.activation(gexp[:, :], gap[:, :], ACT.Exp).then_inc(gexp_ready, 1)

            def chunk(c):
                sc.wait_ge(xcT_done, c + 1)
                nc.scalar.copy(xcT[:, 0, 0, :], bank(7, CHUNK))
                nc.scalar.copy(xcT[0:D2, 0, 1, :], ps[0:D2, 7 * BANK + CHUNK:7 * BANK + 2 * CHUNK]).then_inc(xcT_ready, 1)

            def silu(n, s):
                sc.wait_ge(gu_done, n + 1)
                sc.wait_ge(hid_ready, n - 1) if not (isinstance(n, int) and n < 2) else None
                nc.scalar.activation(act[:, s % 2, :], bank(s % 4, BLK), ACT.Silu).then_inc(act_ready, 1)

            raise_if = None
            SB = 4 * STEPS
            for c in range(4):
                chunk(c)
                for s in range(STEPS):
                    silu(c * STEPS + s, c * STEPS + s)
            with sc.Fori(1, CHUNKS // 4) as i:
                for c in range(4):
                    chunk(4 * i + c)
                    for s in range(STEPS):
                        silu(i * SB + (c * STEPS + s), c * STEPS + s)

        @block.vector
        def _(dve):
            v = nc.vector
            steps = [0]

            def link(ins):
                steps[0] += 1
                ins.then_inc(vchain, 1)
                dve.wait_ge(vchain, steps[0])

            def rsqrt(var):
                link(v.tensor_scalar(rs[0:TOK, 1:2], var, 1.0, EPS, ALU.mult, ALU.add))
                link(v.tensor_scalar(rsi[0:TOK, :], rs[0:TOK, 1:2].bitcast(i32), -0.5, RSQRT_SEED, ALU.mult, ALU.add))
                link(v.tensor_scalar(rs[0:TOK, 1:2], rs[0:TOK, 1:2], -0.5, None, ALU.mult))
                y = rsi[0:TOK, :].bitcast(f32)
                for _ in range(4):
                    link(v.tensor_tensor(rs[0:TOK, 2:3], y, y, ALU.mult))
                    link(v.tensor_scalar(rs[0:TOK, 2:3], rs[0:TOK, 2:3], rs[0:TOK, 1:2], 1.5, ALU.mult, ALU.add))
                    link(v.tensor_tensor(rs[0:TOK, 0:1], y, rs[0:TOK, 2:3], ALU.mult))
                    y = rs[0:TOK, 0:1]

            def normalize(dst, src):
                link(v.bn_stats(bns[0:TOK, :], src))
                link(v.bn_aggr(mv[0:TOK, :], bns[0:TOK, :]))
                rsqrt(mv[0:TOK, 1:2])
                link(v.tensor_scalar(dst, src[0:TOK, 0:dst.shape[1]], mv[0:TOK, 0:1], rs[0:TOK, 0:1], ALU.subtract, ALU.mult))

            def reduce_angle(src):
                link(v.tensor_scalar(ang[0:TOK, 0], src, 1 / (2 * math.pi), MAGIC, ALU.mult, ALU.add))
                link(v.tensor_scalar(ang[0:TOK, 0], ang[0:TOK, 0], MAGIC, None, ALU.subtract))
                link(v.scalar_tensor_tensor(ang[0:TOK, 1], ang[0:TOK, 0], -TWO_PI_A, src, ALU.mult, ALU.add))
                link(v.scalar_tensor_tensor(ang[0:TOK, 2], ang[0:TOK, 0], -TWO_PI_B, ang[0:TOK, 1], ALU.mult, ALU.add))
                link(v.tensor_scalar(ang[0:TOK, 0], ang[0:TOK, 2], -1.0, None, ALU.mult))
                link(v.tensor_tensor(ang[0:TOK, 1], ang[0:TOK, 0], ang[0:TOK, 2], ALU.max))
                v.tensor_scalar(absr[0:TOK, :], ang[0:TOK, 1], math.pi, None, ALU.min).then_inc(abs_ready, 1)

            v.memset(gw[:, :, D:D + 1], 1.0)
            dve.wait_ge(gb_in, 32)
            dve.wait_ge(w_in, 16)
            v.tensor_tensor(gw[:, :, 0:D], wraw, spread(gcol[:, :].rearrange("p (k o) -> p k o", o=1), 2, D),
                            ALU.mult).then_inc(gw_ready, 1)
            dve.wait_ge(pool_consts, 1)
            v.tensor_scalar(ident[:, :], identi[:, :], 0.0, None, ALU.is_equal)
            v.tensor_scalar(before[:, :], identi[:, :], 0.0, None, ALU.is_lt)
            v.tensor_scalar(sel[:, :, :], seli[:, :, :, :].rearrange("p j i r -> p j (i r)"), 0.0, None, ALU.is_equal)
            v.tensor_copy(e_iota[:, :], e_iota_i[:, :])
            v.tensor_copy(c_iota[:, :, :], c_iota_i[:, :, :])
            v.memset(hot[:, :, :, :], 0.0)
            v.memset(cum[:, 0, :], 0.0)
            v.memset(nch[:, :, :], 0.0)
            v.memset(xn[:, :, :], 0.0)
            v.memset(topf[:, :, :], 0.0)
            v.memset(top[:, :, :], 0.0)
            v.tensor_scalar(valid[:, :], validi[:, :], float(NTOK), None, ALU.is_lt).then_inc(vec_consts, 1)
            dve.wait_ge(vec_consts, 1)
            dve.wait_ge(consts_in, N_CONSTS)
            reduce_angle(theta_b[0:TOK, :])
            dve.wait_ge(cos_ready, 1)
            dve.wait_ge(c_bcast, 1)
            v.tensor_copy(c1[:, :], bank(6, D))
            link(v.tensor_tensor(c2[:, :], ps[:, 6 * BANK + D:6 * BANK + 2 * D], bproj_b[:, :], ALU.add))

            for t in range(TILES):
                emb = bank(t % 2, D + 1, TOK)
                dve.wait_ge(tok_done, t + 1)
                dve.wait_ge(ssq_done, t + 1)
                link(v.tensor_scalar(small[0:TOK, 0:1], emb[0:TOK, D:D + 1], -1.0 / KD, None, ALU.mult))
                link(v.tensor_tensor(small[0:TOK, 1:2], small[0:TOK, 0:1], small[0:TOK, 0:1], ALU.mult))
                link(v.scalar_tensor_tensor(small[0:TOK, 2:3], ps[0:TOK, 5 * BANK:5 * BANK + 1], 1.0 / KD, small[0:TOK, 1:2],
                                            ALU.mult, ALU.subtract))
                rsqrt(small[0:TOK, 2:3])
                ins = v.scalar_tensor_tensor(y0[0:TOK, :], c1[0:TOK, :], small[0:TOK, 0:1], emb[0:TOK, 0:D], ALU.mult, ALU.add)
                ins.then_inc(ln1_read, 1)
                dve.wait_ge(ln1_read, t + 1)
                link(v.scalar_tensor_tensor(y1[0:TOK, :], y0[0:TOK, :], rs[0:TOK, 0:1], c2[0:TOK, :], ALU.mult, ALU.add))
                normalize(y0[0:TOK, :], y1[0:TOK, :])
                link(v.tensor_tensor(y1[0:TOK, :], y0[0:TOK, :], ln2g_b[0:TOK, :], ALU.mult))
                link(v.tensor_tensor(h0[0:TOK, :], y1[0:TOK, :], ln2b_b[0:TOK, :], ALU.add))
                normalize(y0[0:TOK, 0:Q], h0[0:TOK, :])
                reduce_angle(y0[0:TOK, 0:Q])
                dve.wait_ge(cos_ready, t + 2)
                v.tensor_tensor(q[0:TOK, :], cosx[0:TOK, :], ctheta[0:TOK, :], ALU.mult).then_inc(q_ready, 1)
                dve.wait_ge(q_ready, t + 1)
                dve.wait_ge(k9_ready, t + 1)
                kh = k9[0:TOK, :, :].rearrange("p j (h d) -> p h j d", d=DK)
                pr = prod[0:TOK, :].rearrange("p (h j d) -> p h j d", h=HEADS, d=DK)
                qh = spread(q[0:TOK, :].rearrange("p (h o d) -> p h o d", o=1, d=DK), 2, SEQ)
                link(v.tensor_tensor(pr, kh, qh, ALU.mult))
                v.tensor_reduce(scores[0:TOK, :].rearrange("p (h j) -> p h j", j=SEQ), pr, AX, ALU.add).then_inc(scores_ready, 1)
                dve.wait_ge(probs_ready, t + 1)
                ph = probs[0:TOK, :].rearrange("p (h j o) -> p h j o", j=SEQ, o=1)
                link(v.tensor_tensor(pr, kh, spread(ph, 3, DK), ALU.mult))
                v.tensor_reduce(mix[0:TOK, :].rearrange("p (h d) -> p h d", d=DK), pr.rearrange("p h j d -> p h d j"), AX, ALU.add)
                link(v.tensor_reduce(den[0:TOK, 0, :], probs[0:TOK, :].rearrange("p (h j) -> p h j", j=SEQ), AX, ALU.add))
                link(v.reciprocal(den[0:TOK, 1, :], den[0:TOK, 0, :]))
                v.tensor_tensor(o[0:TOK, :].rearrange("p (h d) -> p h d", d=DK), mix[0:TOK, :].rearrange("p (h d) -> p h d", d=DK),
                                spread(den[0:TOK, 1, :].rearrange("p (h o) -> p h o", o=1), 2, DK), ALU.mult).then_inc(o_ready, 1)
                dve.wait_ge(proj_done, t + 1)
                link(v.tensor_tensor(h1[0:TOK, t, :], h0[0:TOK, :], ps[0:TOK, 5 * BANK + 64:5 * BANK + 64 + D], ALU.add))
                link(v.bn_stats(bns[0:TOK, :], h1[0:TOK, t, :]))
                link(v.bn_aggr(mv[0:TOK, :], bns[0:TOK, :]))
                rsqrt(mv[0:TOK, 1:2])
                v.tensor_scalar(xn[0:TOK, t, :], h1[0:TOK, t, :], mv[0:TOK, 0:1], rs[0:TOK, 0:1],
                                ALU.subtract, ALU.mult).then_inc(xn_ready, 1)
                dve.wait_ge(logits_done, t + 1)
                v.tensor_copy(logit[0:TOK, :], ps[0:TOK, 5 * BANK + 64 + D:5 * BANK + 64 + D + E]).then_inc(logits_read, 1)
                dve.wait_ge(logits_read, t + 1)
                link(v.max(top[0:TOK, t, :], logit[0:TOK, :]))
                link(v.max_index(topi[0:TOK, t, :], top[0:TOK, t, :], logit[0:TOK, :]))
                link(v.tensor_copy(topf[0:TOK, t, :], topi[0:TOK, t, :]))

            v.tensor_tensor(gap[:, :], top[:, :, 1], top[:, :, 0], ALU.subtract).then_inc(gap_ready, 1)
            eb = spread(e_iota[:, :].rearrange("p (o e) -> p o e", o=1), 1, TILES)
            for k in range(2):
                kb = spread(topf[:, :, k:k + 1], 2, E)
                link(v.tensor_tensor(hot[:, k], eb, kb, ALU.is_equal))
                link(v.tensor_tensor(hot[:, k], hot[:, k], spread(valid[:, :].rearrange("p (t o) -> p t o", o=1), 2, E), ALU.mult))
            v.tensor_tensor(either[:, :, :], hot[:, 0], hot[:, 1], ALU.add).then_inc(either_ready, 1)
            dve.wait_ge(gexp_ready, 1)
            link(v.tensor_scalar(wsel[:, 2, :], gexp[:, :], 1.0, None, ALU.add))
            link(v.reciprocal(wsel[:, 0, :], wsel[:, 2, :]))
            link(v.tensor_tensor(wsel[:, 1, :], wsel[:, 0, :], gexp[:, :], ALU.mult))
            dve.wait_ge(ranks_done, 1)
            te = TILES * E
            link(v.tensor_copy(totals[:, :, :], bank(7, te).rearrange("p (t e) -> p t e", e=E)))
            for t in range(TILES):
                link(v.tensor_tensor(cum[:, t + 1, :], cum[:, t, :], totals[:, t, :], ALU.add))
            for j in range((NTOK + CHUNK - 1) // CHUNK):
                link(v.scalar_tensor_tensor(nch[:, 0, :], cum[:, TILES, :], float(j * CHUNK), nch[:, 0, :], ALU.is_gt, ALU.add))
            link(v.tensor_copy(nch[:, 1, :], nch[:, 0, :]))
            a, b = 1, 2
            for d in (1, 2, 4):
                link(v.tensor_copy(nch[:, b, 0:d], nch[:, a, 0:d]))
                link(v.tensor_tensor(nch[:, b, d:E], nch[:, a, d:E], nch[:, a, 0:E - d], ALU.add))
                a, b = b, a
            ends = nch[:, a, :]
            link(v.tensor_tensor(base[:, :], ends, nch[:, 0, :], ALU.subtract))
            link(v.tensor_tensor(cmp[:, :, :], c_iota[:, :, :], spread(ends.rearrange("p (o e) -> p o e", o=1), 1, CHUNKS), ALU.is_ge))
            link(v.tensor_reduce(cexp[:, :], cmp[:, :, :], AX, ALU.add))
            v.tensor_scalar(cexpi[:, 0, :], cexp[:, :], float(E - 1), None, ALU.min).then_inc(cexp_ready, 1)
            link(v.tensor_tensor(place[:, :, :], ps[:, 7 * BANK + te:7 * BANK + 2 * te].rearrange("p (t e) -> p t e", e=E),
                                 cum[:, 0:TILES, :], ALU.add))
            link(v.scalar_tensor_tensor(place[:, :, :], spread(base[:, :].rearrange("p (o e) -> p o e", o=1), 1, TILES),
                                        float(CHUNK), place[:, :, :], ALU.mult, ALU.add))
            for k in range(2):
                link(v.tensor_tensor(posm[:, k], hot[:, k], place[:, :, :], ALU.mult))
            link(v.tensor_reduce(posf[:, :, :], posm[:, :, :, :], AX, ALU.add))
            v.tensor_copy(posi[:, :, :], posf[:, :, :]).then_inc(pos_ready, 1)

            def gate(n, s):
                dve.wait_ge(act_ready, n + 1)
                if not (isinstance(n, int) and n < 2):
                    dve.wait_ge(hidT_done, n - 1)
                v.tensor_tensor(hid[:, s % 2, :], act[:, s % 2, :], ps[:, (s % 4) * BANK + BLK:(s % 4) * BANK + 2 * BLK],
                                ALU.mult).then_inc(hid_ready, 1)

            def turn(n, s):
                dve.wait_ge(hidT_done, n + 1)
                v.tensor_copy(hidT[:, s % 2], bank(4 + s % 2, BLK).rearrange("p (h t) -> p h t", h=HT)).then_inc(hidT_ready, 1)

            def finish(c, cb):
                dve.wait_ge(down_done, (c + 1))
                if not (isinstance(c, int) and c < 2):
                    dve.wait_ge(y_out[cb], 16 * ((c - cb) // 2) if isinstance(c, int) else 8 * (c - cb))
                v.tensor_copy(yc[:, cb, :], bank(6, D)).then_inc(y_ready, 1)

            def round4(first, c0, n0):
                for s in range(4 * STEPS):
                    gate(n0 + s, s)
                    if not (first and s == 0):
                        turn(n0 + (s - 1), s - 1)
                    c, r = divmod(s, STEPS)
                    if r == 2 and not (first and c == 0):
                        finish(c0 + (c - 1), (c - 1) % 2)

            round4(True, 0, 0)
            with dve.Fori(1, CHUNKS // 4) as i:
                round4(False, 4 * i, i * (4 * STEPS))
            turn(CHUNKS * STEPS - 1, CHUNKS * STEPS - 1)
            finish(CHUNKS - 1, (CHUNKS - 1) % 2)
            for t in range(TILES):
                rows = TOK if t < TILES - 1 else LAST
                dve.wait_ge(gathered, 16 * 2 * TILES)
                link(v.scalar_tensor_tensor(h0[0:rows, :], got[0:rows, 0, t, :], wsel[0:rows, 0, t:t + 1], h1[0:rows, t, :], ALU.mult, ALU.add))
                v.scalar_tensor_tensor(res[0:rows, t, :], got[0:rows, 1, t, :], wsel[0:rows, 1, t:t + 1], h0[0:rows, :], ALU.mult, ALU.add).then_inc(res_ready, 1)
                dve.wait_ge(res_ready, t + 1)

        @block.tensor
        def _(pe):
            mm = nc.tensor.matmul
            pe.wait_ge(gb_in, 32)
            pe.wait_ge(w_in, 16)
            pe.wait_ge(ones_ready, 1)
            for k in range(KT):
                last = mm(ps[0:1, 7 * BANK + D:7 * BANK + 2 * D], bcol[:, k:k + 1], wraw[:, k, :], start=k == 0, stop=k == KT - 1)
            last.then_inc(c_rows, 1)
            pe.wait_ge(gw_ready, 1)
            pe.wait_ge(c_rows, 1)
            for k in range(KT):
                last = mm(ps[0:1, 7 * BANK:7 * BANK + D], ones[:, 0:1], gw[:, k, 0:D], start=k == 0, stop=k == KT - 1)
            last.then_inc(c_rows, 1)

            def embed(t, k0, k1):
                if k0 == 0:
                    pe.wait_ge(x_in[t % 2], 16 * (t // 2 + 1))
                    if t >= 2:
                        pe.wait_ge(ln1_read, t - 1)
                for k in range(k0, k1):
                    last = mm(bank(t % 2, D + 1, TOKP), xbuf[:, t % 2, k, :], gw[:, k, :], start=k == 0, stop=k == KT - 1)
                if k1 == KT:
                    last.then_inc(tok_done, 1)

            def square_sum(t):
                pe.wait_ge(ssq_ready, t + 1)
                if t >= 1:
                    pe.wait_ge(logits_read, t)
                mm(ps[0:TOKP, 5 * BANK:5 * BANK + 1], ssq[:, t % 2, :], ones[:, 0:1], start=True, stop=True).then_inc(ssq_done, 1)

            def gather_images(t):
                pe.wait_ge(q_ready, t + 1)
                if t == 0:
                    pe.wait_ge(vec_consts, 1)
                if t >= 1:
                    pe.wait_ge(k9_ready, t)
                for j in range(SEQ):
                    b, c = (2, j) if j < 5 else (3, j - 5)
                    last = mm(ps[0:TOK, b * BANK + c * Q:b * BANK + (c + 1) * Q], sel[0:TOK, j, :], q[0:TOK, :], start=True, stop=True)
                last.then_inc(k9_done, 1)

            def project(t):
                pe.wait_ge(o_ready, t + 1)
                if t >= 1:
                    pe.wait_ge(xnT_ready, t)
                nc.tensor.transpose(bank(4, TOK, Q), o[0:TOK, :], ident[0:TOK, 0:TOK]).then_inc(oT_done, 1)
                pe.wait_ge(oT_ready, t + 1)
                mm(ps[0:TOK, 5 * BANK + 64:5 * BANK + 64 + D], oT[:, :], wcomb[:, :], start=True, stop=True).then_inc(proj_done, 1)

            def route(t):
                pe.wait_ge(xn_ready, t + 1)
                nc.tensor.transpose(bank(4, TOK), xn[0:TOK, t, 0:P], ident[0:TOK, 0:TOK])
                nc.tensor.transpose(ps[0:D2, 4 * BANK + TOK:4 * BANK + 2 * TOK], xn[0:TOK, t, P:D], ident[0:TOK, 0:TOK]).then_inc(xnT_done, 1)
                pe.wait_ge(xnT_ready, t + 1)
                lg = ps[0:TOK, 5 * BANK + 64 + D:5 * BANK + 64 + D + E]
                mm(lg, xnT[:, 0, :], rt1[:, :], start=True, stop=False)
                mm(lg, xnT[0:D2, 1, :], rt2[:, :], start=False, stop=True).then_inc(logits_done, 1)

            embed(0, 0, KT)
            pe.wait_ge(crow_ready, 1)
            mm(bank(6, 2 * D), ones[0:1, :], crow[:, :, :].rearrange("p a d -> p (a d)"), start=True, stop=True).then_inc(c_bcast, 1)
            G = KT // 4
            pe.wait_ge(consts_in, N_CONSTS)
            for t in range(TILES):
                more = t + 1 < TILES
                if more:
                    embed(t + 1, 0, G)
                square_sum(t)
                if more:
                    embed(t + 1, G, 3 * G)
                gather_images(t)
                if more:
                    embed(t + 1, 3 * G, KT)
                project(t)
                route(t)

            pe.wait_ge(either_ready, 1)
            ev = either[:, :, :].rearrange("p t e -> p (t e)")
            te = TILES * E
            mm(bank(7, te), ones[:, :], ev, start=True, stop=True)
            mm(ps[:, 7 * BANK + te:7 * BANK + 2 * te], before[:, :], ev, start=True, stop=True).then_inc(ranks_done, 1)
            pe.wait_ge(pos_ready, 1)

            w = 2 * HID
            pe.wait_ge(cexp_ready, 1)
            pe.wait_ge(gexp_ready, 1)

            def turn_rows(c, cb):
                pe.wait_ge(xc_in[cb], 8 * (c + (2 - cb)) if not isinstance(c, int) else 16 * (c // 2 + 1))
                if not (isinstance(c, int) and c == 0):
                    pe.wait_ge(xcT_ready, c)
                nc.tensor.transpose(bank(7, CHUNK), xc[:, cb, 0:P], ident[:, :])
                nc.tensor.transpose(ps[0:D2, 7 * BANK + CHUNK:7 * BANK + 2 * CHUNK], xc[:, cb, P:D], ident[:, :]).then_inc(xcT_done, 1)

            def gate_up(n, s, off):
                if not (isinstance(n, int) and n < 4):
                    pe.wait_ge(hid_ready, n - 3)
                r = s % STEPS
                mm(bank(s % 4), xcT[:, 0, 0, :], flat[:, bass.ds(off + 2 * BLK * r, 2 * BLK)], start=True, stop=False)
                mm(bank(s % 4), xcT[0:D2, 0, 1, :], flat[0:D2, bass.ds(off + (w + 2 * BLK * r), 2 * BLK)], start=False, stop=True).then_inc(gu_done, 1)

            def turn_hidden(n, s):
                pe.wait_ge(hid_ready, n + 1)
                if not (isinstance(n, int) and n < 2):
                    pe.wait_ge(hidT_ready, n - 1)
                for h in range(HT):
                    last = nc.tensor.transpose(ps[:, (4 + s % 2) * BANK + h * P:(4 + s % 2) * BANK + (h + 1) * P],
                                               hid[:, s % 2, h * P:(h + 1) * P], ident[:, :])
                last.then_inc(hidT_done, 1)

            def down(c, n, s, off):
                pe.wait_ge(hidT_ready, n + 1)
                r = s % STEPS
                if r == 0 and not (isinstance(c, int) and c == 0):
                    pe.wait_ge(y_ready, c)
                for h in range(HT):
                    k = r * HT + h
                    last = mm(bank(6, D), hidT[:, s % 2, h, :], flat[:, bass.ds(off + (2 * w + k * D), D)],
                              start=k == 0, stop=k == STEPS * HT - 1)
                if r == STEPS - 1:
                    last.then_inc(down_done, 1)

            def expert_of(c):
                e = pe.value_load(cexpi[0:1, 0, bass.ds(c, 1)], min_val=0, max_val=E - 1)
                return e

            regs = [pe.alloc_register(f"expert_off{k}") for k in range(2)]

            def round4(first, c0, n0):
                for s in range(4 * STEPS):
                    c, r = divmod(s, STEPS)
                    if r == 0:
                        e = expert_of(c0 + c)
                        pe.reg_mov(regs[c % 2], e * EW)
                        turn_rows(c0 + c, c % 2)
                        pe.wait_ge(xcT_ready, c0 + (c + 1))
                    here = pe.snap(regs[c % 2], min_val=0, max_val=(E - 1) * EW)
                    if r == 0:
                        pe.wait_ge(experts_ready, pe.snap(e + 1))
                    gate_up(n0 + s, s, here)
                    if not (first and s < 1):
                        turn_hidden(n0 + (s - 1), s - 1)
                    if not (first and s < 2):
                        cd = (s - 2) // STEPS
                        off = pe.snap(regs[cd % 2], min_val=0, max_val=(E - 1) * EW)
                        down(c0 + cd, n0 + (s - 2), s - 2, off)

            round4(True, 0, 0)
            with pe.Fori(1, CHUNKS // 4) as i:
                round4(False, 4 * i, i * (4 * STEPS))
            S = CHUNKS * STEPS
            off = pe.snap(regs[(CHUNKS - 1) % 2], min_val=0, max_val=(E - 1) * EW)
            down(CHUNKS - 1, S - 2, S - 2, off)
            turn_hidden(S - 1, S - 1)
            down(CHUNKS - 1, S - 1, S - 1, off)


def kernel(x, L0_tok_ln1_g, L0_tok_ln1_b, L0_tok_W_proj, L0_tok_b_proj, L0_tok_ln2_g, L0_tok_ln2_b,
           L0_attn_theta, L0_attn_W_combine, L0_ffn_router_w, L0_ffn_Wg, L0_ffn_Wu, L0_ffn_Wd):
    import numpy as np
    import concourse.bacc as bacc
    from concourse.bass_utils import run_bass_kernel_spmd

    P, PATCH, SEQ, IMGS, TILES, BLK = 128, 32, 9, 13, 5, 256
    x = np.asarray(x)
    B, C, H, W = x.shape
    tok = x.reshape(B, C, H // PATCH, PATCH, W // PATCH, PATCH).transpose(0, 2, 4, 3, 5, 1).reshape(B * SEQ, -1)
    K = tok.shape[1]
    KT = K // P
    TOK = IMGS * SEQ
    full = np.zeros((TILES * TOK, K), tok.dtype)
    full[:B * SEQ] = tok
    xt = np.ones((TILES, P, KT, TOK + 1), tok.dtype)
    xt[..., :TOK] = full.reshape(TILES, TOK, P, KT).transpose(0, 2, 3, 1)
    Wg, Wu, Wd = (np.asarray(a) for a in (L0_ffn_Wg, L0_ffn_Wu, L0_ffn_Wd))
    E, HID, D = Wg.shape
    gu = np.stack([Wg.transpose(0, 2, 1).reshape(E, D, HID // BLK, BLK),
                   Wu.transpose(0, 2, 1).reshape(E, D, HID // BLK, BLK)], axis=3).reshape(E, D, 2 * HID)
    wd = Wd.transpose(0, 2, 1).reshape(E, HID // P, P, D).transpose(0, 2, 1, 3).reshape(E, P, -1)
    ins = {
        "x_t": xt,
        "ln1_g": np.asarray(L0_tok_ln1_g).reshape(P, KT), "ln1_b": np.asarray(L0_tok_ln1_b).reshape(P, KT),
        "w_proj": np.asarray(L0_tok_W_proj), "b_proj": np.asarray(L0_tok_b_proj),
        "ln2_g": np.asarray(L0_tok_ln2_g), "ln2_b": np.asarray(L0_tok_ln2_b),
        "theta": np.asarray(L0_attn_theta), "w_comb": np.asarray(L0_attn_W_combine).T,
        "router": np.asarray(L0_ffn_router_w).T,
        "w_k1": gu[:, :P], "w_k2": gu[:, P:], "w_down": wd,
    }
    ins = {k: np.ascontiguousarray(a) for k, a in ins.items()}
    nc = bacc.Bacc("TRN2", target_bir_lowering=False, num_devices=1)
    args = [nc.dram_tensor(k, a.shape, mybir.dt.from_np(a.dtype), kind="ExternalInput").ap() for k, a in ins.items()]
    args.append(nc.dram_tensor("out", (B * SEQ, D), mybir.dt.float32, kind="ExternalOutput").ap())
    chunks = (2 * B * SEQ + E * (P - 1)) // P
    args.append(nc.dram_tensor("slot_x", (chunks * P, D), mybir.dt.float32, kind="Internal").ap())
    args.append(nc.dram_tensor("slot_y", (chunks * P, D), mybir.dt.float32, kind="Internal").ap())
    vit_tower(nc, *args)
    r = run_bass_kernel_spmd(nc, [ins], core_ids=[0])
    return r.results[0]["out"].reshape(B, SEQ, D)
```

```python
import math
from contextlib import ExitStack

import concourse.bass as bass
from concourse import mybir


def vit_tower(nc, x, ln1_g, ln1_b, w_proj, b_proj, ln2_g, ln2_b, theta, w_comb, router,
              w_exp, out, slot_x, pair_y):
    f32 = mybir.dt.float32
    f16 = mybir.dt.float16
    bf16 = mybir.dt.bfloat16
    i32 = mybir.dt.int32
    u32 = mybir.dt.uint32
    ALU = mybir.AluOpType
    ACT = mybir.ActivationFunctionType
    AX = mybir.AxisListType.X

    TILES, P, KT, TOK = x.shape
    D = w_proj.shape[1]
    D2 = D - P
    KD = KT * P
    SEQ = 9
    IMGS = TOK // SEQ
    NTOK = out.shape[0]
    LAST = NTOK - (TILES - 1) * TOK
    Q = theta.shape[0]
    HEADS = 12
    DK = Q // HEADS
    HB = 4
    HA = HEADS // HB
    DX = DK + 1
    E, _, EW = w_exp.shape
    HID = 768
    W2 = 2 * HID
    BLK = 256
    STEPS = HID // BLK
    HT = BLK // P
    CHUNK = P
    CHUNKS = (2 * NTOK + E * (CHUNK - 1)) // CHUNK
    ROW = D + (P - D2) + 1
    NP = 4
    PW = EW // NP
    STAGES = 3
    GROUPS = [(0, 3), (3, 5)]
    EPS = 1e-5
    BIG = 512.0
    MAGIC = 1.5 * 2.0 ** 23
    TWO_PI_A = 6.28125
    TWO_PI_B = 2 * math.pi - TWO_PI_A
    RSQRT_SEED = float(0x5F3759DF)
    EARLY = 4

    def spread(ap, dim, n):
        shape = list(ap.shape)
        shape[dim] = n
        return ap.broadcast_to(shape)

    ctx = ExitStack()
    with ctx:
        def sb(name, shape, dt=f32):
            return ctx.enter_context(nc.sbuf_tensor(name, shape, dt))

        def sem(name):
            return ctx.enter_context(nc.semaphore(name))

        experts = sb("experts", [P, E * EW])
        flat = experts[:, :]
        hi_w = flat.bitcast(f16)
        lo_w = flat.bitcast(bf16)
        at = EARLY * EW
        gw = flat[:, at:at + KT * (D + 1)].rearrange("p (k d) -> p k d", k=KT)
        at += KT * (D + 1)
        xbuf = flat[:, at:at + 2 * KT * TOK].rearrange("p (b k t) -> p b k t", b=2, k=KT)
        at += 2 * KT * TOK
        GS = 4
        NG = KT // GS
        sq = flat[:, at:at + 2 * GS * TOK].rearrange("p (b k t) -> p b k t", b=2, k=GS)
        at += 2 * GS * TOK
        ssq = flat[:, at:at + 2 * GS * TOK].rearrange("p (b k t) -> p b k t", b=2, k=GS)
        at += 2 * GS * TOK

        def carve(size, dt=f32):
            nonlocal at
            at += size
            assert at <= E * EW
            return flat[:, at - size:at].bitcast(dt)

        diff = carve(P, i32)
        part = carve(TOK, i32)
        imgd = carve(TOK, i32).rearrange("p (i r) -> p i r", i=IMGS)
        mask_f = carve(3 * TOK).rearrange("p (a t) -> p a t", a=3)
        blank = carve(ROW - 1)
        spare_pair = carve(CHUNKS, i32)
        theta_b = carve(Q)
        e_iota_i = carve(E, i32)
        c_iota_i = carve(CHUNKS * E, i32).rearrange("p (c e) -> p c e", e=E)
        m_iota_i = carve(E * TILES, i32).rearrange("p (e t) -> p e t", e=E)
        wraw = flat[:, 2 * EW:2 * EW + KT * D].rearrange("p (k d) -> p k d", k=KT)
        stage = sb("stage", [P, STAGES, PW])
        gcol = sb("gcol", [P, KT])
        bcol = sb("bcol", [P, KT])
        ones = sb("ones", [P, P])
        ones_b = sb("ones_b", [P, P], bf16)
        ident = sb("ident", [P, P])
        ident_h = sb("ident_h", [P, P], f16)
        before = sb("before", [P, P], bf16)
        mask = sb("mask", [P, 2, TOK], f16)
        e_iota = sb("e_iota", [P, E])
        c_iota = sb("c_iota", [P, CHUNKS, E])
        m_iota = sb("m_iota", [P, E, TILES])
        pow8 = sb("pow8", [P, 2, CHUNKS // 2])
        validi = sb("validi", [P, TILES], i32)
        valid = sb("valid", [P, TILES])
        ln2g_b = sb("ln2g_b", [P, D])
        ln2b_b = sb("ln2b_b", [P, D])
        bproj_b = sb("bproj_b", [P, D])
        wcomb = sb("wcomb", [Q, D])
        rt1 = sb("rt1", [P, E])
        rt2 = sb("rt2", [D2, E])
        halfpi = sb("halfpi", [P, 1])
        ctheta = sb("ctheta", [P, Q])
        c1 = sb("c1", [P, D])
        c2 = sb("c2", [P, D])
        small = sb("small", [P, 3, TILES])
        bns = sb("bns", [P, TILES, 6])
        mv = sb("mv", [P, TILES, 2])
        rs = sb("rs", [P, 3, TILES])
        rsi = sb("rsi", [P, TILES], i32)
        yy = sb("yy", [P, 2, TILES, D])
        y0 = yy[:, 0]
        y1 = yy[:, 1]
        h0 = sb("h0", [P, TILES, D])
        h1 = sb("h1", [P, TILES, D])
        qx = sb("qx", [P, TILES, HEADS, DX])
        qh = sb("qh", [P, 2, 3, Q], f16)
        QAB = 3 * 2 * HEADS * 4 * DK // 2
        PRB = HB * HA * TOK
        ANG = 3 * 3 * Q
        shared = sb("shared", [P, QAB + PRB + ANG])
        qab = shared[:, 0:QAB].bitcast(f16).rearrange("p (t s h r d) -> p t s h r d", t=3, s=2, h=HEADS, r=4)
        probs = shared[:, QAB:QAB + PRB].rearrange("p (b a t) -> p b a t", b=HB, a=HA)
        csum = h1[:, 0:2, :]
        ang = shared[:, QAB + PRB:QAB + PRB + ANG].rearrange("p (i t q) -> p i t q", i=3, t=3)
        TP = TOK + 1
        qabT = sb("qabT", [P, 2 * HA, TP], f16)
        rden = sb("rden", [P, 3, HEADS])
        o = sb("o", [P, 3, Q])
        oT = sb("oT", [Q, 3, TOK])
        xs = sb("xs", [P, TILES, 2, ROW])
        xnT = sb("xnT", [P, 2, 3, TOK])
        top = sb("top", [P, TILES, 8])
        logit = sb("logit", [P, TILES, E])
        topi = sb("topi", [P, TILES, 8], u32)
        topf = sb("topf", [P, TILES, 8])
        gap = sb("gap", [P, TILES])
        gexp = sb("gexp", [P, TILES])
        wsel = sb("wsel", [P, 3, TILES])
        hot = sb("hot", [P, 2, TILES, E])
        either = sb("either", [P, TILES + 1, E], bf16)
        place = sb("place", [P, TILES + 1, E])
        full = sb("full", [P, E, TILES])
        nch = sb("nch", [P, 3, E])
        base = sb("base", [P, E])
        posm = sb("posm", [P, 2, TILES, E])
        posf = sb("posf", [P, 2, TILES])
        posi = sb("posi", [P, 2, TILES], u32)
        cmp = sb("cmp", [P, CHUNKS, E])
        cexp = sb("cexp", [P, 2, CHUNKS // 2])
        words = sb("words", [P, 2])
        wordsi = sb("wordsi", [P, 2], i32)
        at2 = 0

        def reuse_shared(words, dt=f32):
            nonlocal at2
            at2 += words
            assert at2 <= QAB + PRB + ANG
            return shared[:, at2 - words:at2].bitcast(dt)

        xc = reuse_shared(4 * ROW).rearrange("p (j w) -> p j w", j=4)
        x1h = reuse_shared(2 * CHUNK, f16).rearrange("p (j k t) -> p j k t", j=2, k=2)
        x1l = reuse_shared(CHUNK, f16).rearrange("p (j t) -> p j t", j=2)
        act = reuse_shared(2 * BLK).rearrange("p (j n) -> p j n", j=2)
        hid = reuse_shared(2 * BLK).rearrange("p (j n) -> p j n", j=2)
        hh = reuse_shared(BLK, f16).rearrange("p (j h t) -> p j h t", j=2, h=HT)
        hl = reuse_shared(BLK, bf16).rearrange("p (j h t) -> p j h t", j=2, h=HT)
        yc = reuse_shared(2 * D).rearrange("p (j d) -> p j d", j=2)
        got = yy

        BANK = 512
        ps = ctx.enter_context(nc.psum_tensor("ps", [P, 8 * BANK], f32))

        def pcol(b, off, n, rows=P):
            return ps[0:rows, b * BANK + off:b * BANK + off + n]

        Y_BANKS = (3, 6)
        ps_qT = pcol(7, 0, BANK).bitcast(f16)

        def emb_at(t):
            return t * 256 if t < GROUPS[0][1] else 2 * BANK + (t - GROUPS[0][1]) * 256

        def ssq_at(t):
            return 7 * BANK + 400 + t

        w_in = [sem(f"w_in{j}") for j in range(4)]
        x0_in = [sem(f"x0_in{j}") for j in range(4)]
        x_in = [sem("x_in0"), sem("x_in1")]
        gain_in = sem("gain_in")
        bias_in = sem("bias_in")
        consts_in = sem("consts_in")
        stage_in = [sem(f"stage_in{j}") for j in range(STAGES)]
        hi_done = sem("hi_done")
        split_done = sem("split_done")
        blank_out = sem("blank_out")
        pool_consts = sem("pool_consts")
        vec_consts = sem("vec_consts")
        gw_ready = sem("gw_ready")
        csum_ready = sem("csum_ready")
        c_bcast = sem("c_bcast")
        sq_ready = sem("sq_ready")
        sq_used = sem("sq_used")
        ssq_ready = sem("ssq_ready")
        ssq_done = sem("ssq_done")
        tok_done = sem("tok_done")
        abs_ready = sem("abs_ready")
        cos_ready = sem("cos_ready")
        q_ready = sem("q_ready")
        qhl_ready = sem("qhl_ready")
        qab_ready = sem("qab_ready")
        qT_done = sem("qT_done")
        qT_ready = sem("qT_ready")
        scores_done = sem("scores_done")
        probs_ready = sem("probs_ready")
        pv_done = sem("pv_done")
        o_ready = sem("o_ready")
        oT_done = sem("oT_done")
        oT_ready = sem("oT_ready")
        proj_done = sem("proj_done")
        xn_ready = sem("xn_ready")
        xs_ready = sem("xs_ready")
        xnT_done = sem("xnT_done")
        xnT_ready = sem("xnT_ready")
        logits_done = sem("logits_done")
        logits_read = sem("logits_read")
        gap_ready = sem("gap_ready")
        gexp_ready = sem("gexp_ready")
        either_ready = sem("either_ready")
        ranks_done = sem("ranks_done")
        pos_ready = sem("pos_ready")
        words_ready = sem("words_ready")
        scattered = sem("scattered")
        xc_in = [sem(f"xc_in{j}") for j in range(4)]
        xcT_done = sem("xcT_done")
        xh_ready = sem("xh_ready")
        xcT_ready = sem("xcT_ready")
        gu_done = sem("gu_done")
        act_ready = sem("act_ready")
        hid_ready = sem("hid_ready")
        hidT_done = sem("hidT_done")
        hh_ready = sem("hh_ready")
        hidT_ready = sem("hidT_ready")
        down_done = sem("down_done")
        y_ready = sem("y_ready")
        y_out = [sem("y_out0"), sem("y_out1")]
        got_in = sem("got_in")
        res_ready = sem("res_ready")
        out_done = sem("out_done")
        vchain = sem("vchain")
        pchain = sem("pchain")

        N_CONSTS = 7 * 16
        KC = KT // 4

        def wait_x(eng, t, j):
            if t == 0:
                eng.wait_ge(x0_in[j], 16)
            else:
                eng.wait_ge(x_in[t % 2], 16 * ((t + 1) // 2))

        block = ctx.enter_context(nc.Block())

        @block.sync
        def _(sp):
            def load_x(t):
                if t >= 2:
                    sp.wait_ge(tok_done, t - 1)
                    sp.wait_ge(sq_ready, NG * (t - 1))
                sp.dma_start(xbuf[:, t % 2], x[t]).then_inc(x_in[t % 2], 16)

            def load_piece(n):
                e, j = divmod(n, NP)
                k = n % STAGES
                if n >= STAGES:
                    sp.wait_ge(split_done, n - STAGES + 1)
                sp.dma_start(stage[:, k, :], w_exp[e, :, j * PW:(j + 1) * PW]).then_inc(stage_in[k], 16)

            sp.dma_start(gcol[:, :], ln1_g).then_inc(gain_in, 16)
            wsrc = w_proj.rearrange("(p k) d -> p k d", p=P)
            for j in range(4):
                ks = slice(j * KC, (j + 1) * KC)
                sp.dma_start(wraw[:, ks, :], wsrc[:, ks, :]).then_inc(w_in[j], 16)
                sp.dma_start(xbuf[:, 0, ks, :], x[0, :, ks, :]).then_inc(x0_in[j], 16)
            sp.dma_start(bcol[:, :], ln1_b).then_inc(bias_in, 16)
            for dst, src in ((theta_b, theta), (ln2g_b, ln2_g), (ln2b_b, ln2_b), (bproj_b, b_proj)):
                sp.dma_start(dst[:, :], spread(src.rearrange("(o n) -> o n", o=1), 0, P)).then_inc(consts_in, 16)
            sp.dma_start(wcomb[:, :], w_comb).then_inc(consts_in, 16)
            sp.dma_start(rt1[:, :], router[0:P, :]).then_inc(consts_in, 16)
            sp.dma_start(rt2[:, :], router[P:D, :]).then_inc(consts_in, 16)
            load_x(1)
            for n in range(0, 3):
                load_piece(n)
            load_x(2)
            load_x(3)
            for n in range(3, 6):
                load_piece(n)
            load_x(4)
            sp.wait_ge(pool_consts, 1)
            slots = slot_x.rearrange("(c p) w -> p c w", p=CHUNK)
            sp.dma_start(slots[:, :, 0:ROW - 1], spread(blank[:, :].rearrange("p (o w) -> p o w", o=1), 1, CHUNKS)).then_inc(blank_out, 16)
            sp.dma_start(slots[:, :, ROW - 1:ROW].bitcast(i32), spare_pair[:, :].rearrange("p (c o) -> p c o", o=1),
                         allow_slow_non_contiguous=True).then_inc(blank_out, 16)
            for n in range(6, NP * E):
                load_piece(n)

            sp.wait_ge(scattered, 16 * 2 * TILES)

            def load_chunk(c, j, reuse):
                if reuse:
                    sp.wait_ge(y_out[j % 2], 8 * (c - j) + (16 * (j // 2) - 16))
                sp.dma_start(xc[:, j, :], slot_x[bass.ts(c, CHUNK), :]).then_inc(xc_in[j], 16)

            for j in range(4):
                load_chunk(j, j, False)
            with sp.Fori(1, CHUNKS // 4) as i:
                for j in range(4):
                    load_chunk(4 * i + j, j, True)
            for k in range(2):
                sp.wait_ge(y_out[k], 16 * (CHUNKS // 2))
            for a, n, rows in ((0, TILES - 1, TOK), (TILES - 1, 1, LAST)):
                for k in range(2):
                    r0 = k * NTOK + a * TOK
                    sp.dma_start(got[0:rows, k, a:a + n, :],
                                 pair_y[r0:r0 + n * rows, :].rearrange("(t p) d -> p t d", p=rows)).then_inc(got_in, 16)
            sp.wait_ge(res_ready, TILES)
            for a, n, rows in ((0, TILES - 1, TOK), (TILES - 1, 1, LAST)):
                sp.dma_start(out[a * TOK:a * TOK + n * rows, :].rearrange("(t p) d -> p t d", p=rows),
                             h0[0:rows, a:a + n, :]).then_inc(out_done, 16)
            sp.wait_ge(out_done, 32)

        @block.gpsimd
        def _(pool):
            steps = [0]

            def link(ins):
                steps[0] += 1
                ins.then_inc(pchain, 1)
                pool.wait_ge(pchain, steps[0])

            g = nc.gpsimd
            g.memset(ones[:, :], 1.0)
            g.memset(halfpi[:, :], math.pi / 2)
            g.memset(blank[:, :], 0.0)
            g.memset(ones_b[:, :], 1.0)
            g.memset(qx[:, :, :, :], 1.0)
            for c in range(CHUNKS // 2):
                g.memset(pow8[:, :, c:c + 1], 8.0 ** c)
            link(g.iota(diff[:, :], pattern=[[-1, P]], base=0, channel_multiplier=1))
            for b in range(HB):
                r = slice(32 * b, 32 * b + 32)
                link(g.iota(part[r, :], pattern=[[0, TOK]], base=0, channel_multiplier=1))
                link(g.iota(imgd[r, :, :], pattern=[[1, IMGS], [0, SEQ]], base=0, channel_multiplier=-1))
            g.iota(e_iota_i[:, :], pattern=[[1, E]], base=0, channel_multiplier=0)
            g.iota(c_iota_i[:, :, :], pattern=[[1, CHUNKS], [0, E]], base=0, channel_multiplier=0)
            g.iota(m_iota_i[:, :, :], pattern=[[0, E], [CHUNK, TILES]], base=0, channel_multiplier=0)
            for t in range(TILES):
                for k in range(2):
                    g.iota(xs[:, t, k, ROW - 1:ROW].bitcast(i32), pattern=[[0, 1]], base=k * NTOK + t * TOK, channel_multiplier=1)
            g.iota(validi[:, :], pattern=[[TOK, TILES]], base=0, channel_multiplier=1)
            g.iota(spare_pair[:, :], pattern=[[CHUNK, CHUNKS]], base=2 * NTOK, channel_multiplier=1).then_inc(pool_consts, 1)
            for t in range(TILES):
                acc = ssq[:, t % 2]
                for j in range(1, NG):
                    n = NG * t + j
                    pool.wait_ge(sq_ready, n + 1)
                    added = (NG - 1) * t + j
                    g.tensor_tensor(acc, acc, sq[:, added % 2], ALU.add).then_inc(sq_used, 1)
                    pool.wait_ge(sq_used, added)
                g.tensor_tensor(acc[:, 0:2], acc[:, 0:2], acc[:, 2:4], ALU.add).then_inc(ssq_ready, 1)
            pool.wait_ge(blank_out, 32)
            pool.wait_ge(xs_ready, 2)
            pool.wait_ge(pos_ready, 1)
            for t in range(TILES):
                rows = TOK if t < TILES - 1 else LAST
                for k in range(2):
                    pool.indirect_dma_start(
                        out=slot_x, out_offset=bass.IndirectOffsetOnAxis(ap=posi[0:rows, k, t:t + 1], axis=0),
                        in_=xs[0:rows, t, k, :], in_offset=None).then_inc(scattered, 16)

            for c in range(CHUNKS):
                pool.wait_ge(y_ready, c + 1)
                pool.indirect_dma_start(
                    out=pair_y, out_offset=bass.IndirectOffsetOnAxis(ap=xc[:, c % 4, ROW - 1:ROW].bitcast(u32), axis=0),
                    in_=yc[:, c % 2, :], in_offset=None).then_inc(y_out[c % 2], 16)

        @block.scalar
        def _(sc):
            a = nc.scalar

            def squares(t, j0, j1):
                for j in range(j0, j1):
                    n = NG * t + j
                    wait_x(sc, t, j * GS // KC)
                    if j == 0 and t >= 2:
                        sc.wait_ge(ssq_done, t - 1)
                    if j > 0 and (NG - 1) * t + j > 2:
                        sc.wait_ge(sq_used, (NG - 1) * t + j - 2)
                    dst = ssq[:, t % 2] if j == 0 else sq[:, ((NG - 1) * t + j) % 2]
                    a.activation(dst, xbuf[:, t % 2, j * GS:(j + 1) * GS, :], ACT.Square).then_inc(sq_ready, 1)

            def high_part(n):
                e, j = divmod(n, NP)
                to = 2 * e * EW + j * PW
                if n == NP * 2:
                    sc.wait_ge(csum_ready, 1)
                if n == NP * EARLY:
                    sc.wait_ge(tok_done, TILES)
                    sc.wait_ge(ssq_done, TILES)
                    sc.wait_ge(blank_out, 32)
                sc.wait_ge(stage_in[n % STAGES], 16 * (n // STAGES + 1))
                a.copy(hi_w[:, to:to + PW], stage[:, n % STAGES, :]).then_inc(hi_done, 1)

            def cosine(n, dst, src):
                sc.wait_ge(abs_ready, n + 1)
                a.activation(dst, src, ACT.Sin, bias=halfpi[0:TOK, 0:1], scale=-1.0).then_inc(cos_ready, 1)

            def attend(t):
                sc.wait_ge(qT_done, t + 1)
                a.copy(qabT[:, :, 0:TOK], ps_qT[:, 0:2 * HA * TP].rearrange("p (g t) -> p g t", t=TP)[:, :, 0:TOK]).then_inc(qT_ready, 1)
                sc.wait_ge(scores_done, t + 1)
                if t >= 1:
                    sc.wait_ge(pv_done, t)
                a.activation(probs[0:TOK].rearrange("p b a t -> p b (a t)"),
                             ps[0:TOK, 3 * BANK:7 * BANK].rearrange("p (b n) -> p b n", b=HB)[:, :, 0:HA * TOK],
                             ACT.Exp, scale=DK ** -0.5).then_inc(probs_ready, 1)

            def after(g):
                t0, t1 = GROUPS[g]
                n = t1 - t0
                sc.wait_ge(oT_done, g + 1)
                a.copy(oT[:, 0:n, :], pcol(1, 0, n * TOK, Q).rearrange("p (t c) -> p t c", t=n)).then_inc(oT_ready, 1)
                sc.wait_ge(xn_ready, g + 1)
                sc.wait_ge(xnT_done, g + 1)
                a.copy(xnT[:, 0, 0:n, :], pcol(5, 0, n * TOK).rearrange("p (t c) -> p t c", t=n))
                a.copy(xnT[0:D2, 1, 0:n, :], pcol(6, 0, n * TOK, D2).rearrange("p (t c) -> p t c", t=n)).then_inc(xnT_ready, 1)
                for k in range(2):
                    if k:
                        a.copy(xs[0:TOK, t0:t1, k, 0:D], xs[0:TOK, t0:t1, 0, 0:D])
                    last = a.copy(xs[0:TOK, t0:t1, k, D:ROW - 1], xs[0:TOK, t0:t1, 0, P:D])
                last.then_inc(xs_ready, 1)

            sc.wait_ge(pool_consts, 1)
            squares(0, 0, NG)
            cosine(0, ctheta[0:TOK, :], ang[0:TOK, 0, 0, :])
            for t in range(1, TILES):
                for j in range(0, NG, 4):
                    squares(t, j, j + 4)
                    if t > 1 and j:
                        for n in range(3 * (t - 2), 3 * (t - 1)):
                            high_part(n)
            cosine(1, ang[0:TOK, 1], ang[0:TOK, 0])
            attend(0)
            for n in range(9, 12):
                high_part(n)
            attend(1)
            attend(2)
            for n in range(12, 15):
                high_part(n)
            after(0)
            high_part(15)
            cosine(2, ang[0:TOK, 1, 0:2], ang[0:TOK, 0, 0:2])
            attend(3)
            attend(4)
            for n in range(16, 20):
                high_part(n)
            after(1)
            sc.wait_ge(gap_ready, 1)
            a.activation(gexp[:, :], gap[:, :], ACT.Exp).then_inc(gexp_ready, 1)
            for n in range(20, NP * E):
                high_part(n)

            def silu(n, s):
                sc.wait_ge(gu_done, n + 1)
                if not (isinstance(n, int) and n < 2):
                    sc.wait_ge(hid_ready, n - 1)
                a.activation(act[:, s % 2, :], pcol(s % 3, 0, BLK), ACT.Silu).then_inc(act_ready, 1)

            def hidden_high(n, s):
                sc.wait_ge(hidT_done, n + 1)
                a.copy(hh[:, s % 2], pcol(4 + s % 2, 0, BLK).rearrange("p (h t) -> p h t", h=HT)).then_inc(hh_ready, 1)

            def rows_high(c, j):
                sc.wait_ge(xcT_done, c + 1)
                a.copy(x1h[:, j % 2], pcol(7, 0, 2 * CHUNK).rearrange("p (k t) -> p k t", k=2)).then_inc(xh_ready, 1)

            def round4(first, last, c0, n0):
                for s in range(4 * STEPS):
                    j, r = divmod(s, STEPS)
                    silu(n0 + s, s)
                    if not (first and s == 0):
                        hidden_high(n0 + (s - 1), s - 1)
                    if r == 1 and not (last and j == 3):
                        rows_high(c0 + (j + 1), j + 1)

            rows_high(0, 0)
            round4(True, False, 0, 0)
            with sc.Fori(1, CHUNKS // 4 - 1) as i:
                round4(False, False, 4 * i, i * (4 * STEPS))
            round4(False, True, CHUNKS - 4, (CHUNKS - 4) * STEPS)
            hidden_high(CHUNKS * STEPS - 1, CHUNKS * STEPS - 1)

        @block.vector
        def _(dve):
            v = nc.vector
            steps = [0]

            def link(ins):
                steps[0] += 1
                ins.then_inc(vchain, 1)
                dve.wait_ge(vchain, steps[0])

            def low_part(n):
                e, j = divmod(n, NP)
                to = 2 * e * EW + j * PW
                dve.wait_ge(hi_done, n + 1)
                v.tensor_tensor(lo_w[:, to + EW:to + EW + PW], stage[:, n % STAGES, :], hi_w[:, to:to + PW], ALU.subtract).then_inc(split_done, 1)

            def rsqrt(var, t0, t1):
                vv, y, w = (rs[0:TOK, i, t0:t1] for i in (1, 0, 2))
                link(v.tensor_scalar(vv, var, 1.0, EPS, ALU.mult, ALU.add))
                link(v.tensor_scalar(rsi[0:TOK, t0:t1], vv.bitcast(i32), -0.5, RSQRT_SEED, ALU.mult, ALU.add))
                at = rsi[0:TOK, t0:t1].bitcast(f32)
                for _ in range(3):
                    link(v.scalar_tensor_tensor(w, at, -0.5, at, ALU.mult, ALU.mult))
                    link(v.tensor_tensor(w, w, vv, ALU.mult))
                    link(v.scalar_tensor_tensor(y, w, 1.5, at, ALU.add, ALU.mult))
                    at = y

            def normalize(dst, src, t0, t1):
                for t in range(t0, t1):
                    last = v.bn_stats(bns[0:TOK, t, :], src(t))
                link(last)
                for t in range(t0, t1):
                    last = v.bn_aggr(mv[0:TOK, t, :], bns[0:TOK, t, :])
                link(last)
                rsqrt(mv[0:TOK, t0:t1, 1], t0, t1)
                for t in range(t0, t1):
                    d = dst(t)
                    last = v.tensor_scalar(d, src(t)[:, 0:d.shape[1]], mv[0:TOK, t, 0:1], rs[0:TOK, 0, t:t + 1], ALU.subtract, ALU.mult)
                return last

            def reduce_angle(src, dst):
                link(v.tensor_scalar(dst(0), src, 1 / (2 * math.pi), MAGIC, ALU.mult, ALU.add))
                v.tensor_scalar(dst(1), dst(0), MAGIC, -TWO_PI_A, ALU.subtract, ALU.mult)
                link(v.tensor_scalar(dst(2), dst(0), MAGIC, -TWO_PI_B, ALU.subtract, ALU.mult))
                link(v.tensor_tensor(dst(0), dst(1), src, ALU.add))
                link(v.tensor_tensor(dst(1), dst(0), dst(2), ALU.add))
                v.scalar_tensor_tensor(dst(0), dst(1), -1.0, dst(1), ALU.mult, ALU.max).then_inc(abs_ready, 1)

            dve.wait_ge(gain_in, 16)
            v.memset(gw[:, :, D:D + 1], 1.0)
            for j in range(4):
                dve.wait_ge(w_in[j], 16)
                ks = slice(j * KC, (j + 1) * KC)
                v.tensor_tensor(gw[:, ks, 0:D], wraw[:, ks, :], spread(gcol[:, ks].rearrange("p (k o) -> p k o", o=1), 2, D),
                                ALU.mult).then_inc(gw_ready, 1)
            dve.wait_ge(pool_consts, 1)
            v.tensor_scalar(ident[:, :], diff[:, :], 0.0, None, ALU.is_equal)
            v.tensor_scalar(ident_h[:, :], diff[:, :], 0.0, None, ALU.is_equal)
            v.tensor_scalar(before[:, :], diff[:, :], 0.0, None, ALU.is_lt)
            img = imgd[:, :, :].rearrange("p i r -> p (i r)")
            v.tensor_scalar(mask_f[:, 0, :], img, 0.0, None, ALU.is_equal)
            link(v.tensor_scalar(mask_f[:, 1, :], img, 0.0, BIG, ALU.is_equal, ALU.mult))
            v.scalar_tensor_tensor(mask[:, 0, :], part[:, :], float(IMGS), mask_f[:, 0, :], ALU.is_equal, ALU.add)
            link(v.tensor_scalar(mask_f[:, 2, :], part[:, :], float(IMGS), -BIG, ALU.is_equal, ALU.mult))
            v.tensor_tensor(mask[:, 1, :], mask_f[:, 2, :], mask_f[:, 1, :], ALU.add)
            v.tensor_copy(e_iota[:, :], e_iota_i[:, :])
            v.tensor_copy(c_iota[:, :, :], c_iota_i[:, :, :])
            v.tensor_copy(m_iota[:, :, :], m_iota_i[:, :, :])
            v.memset(either[:, TILES, :], 0.0)
            v.memset(topf[:, :, :], 0.0)
            v.memset(top[:, :, :], 0.0)
            v.tensor_scalar(valid[:, :], validi[:, :], float(NTOK), None, ALU.is_lt).then_inc(vec_consts, 1)
            dve.wait_ge(vec_consts, 1)
            dve.wait_ge(consts_in, N_CONSTS)
            reduce_angle(theta_b[0:TOK, :], lambda i: ang[0:TOK, i, 0, :])
            dve.wait_ge(bias_in, 16)
            v.tensor_reduce(csum[:, 0, :], gw[:, :, 0:D].rearrange("p k d -> p d k"), AX, ALU.add)
            link(v.tensor_tensor(wraw, wraw, spread(bcol[:, :].rearrange("p (k o) -> p k o", o=1), 2, D), ALU.mult))
            v.tensor_reduce(csum[:, 1, :], wraw.rearrange("p k d -> p d k"), AX, ALU.add).then_inc(csum_ready, 1)
            for n in range(0, 6):
                low_part(n)
            dve.wait_ge(c_bcast, 1)
            v.tensor_copy(c1[:, :], pcol(6, 0, D))
            link(v.tensor_tensor(c2[:, :], pcol(6, D, D), bproj_b[:, :], ALU.add))

            def front(g):
                t0, t1 = GROUPS[g]
                n = t1 - t0
                dve.wait_ge(tok_done, t1)
                dve.wait_ge(ssq_done, t1)
                nm, msq, var = (small[0:TOK, i, t0:t1] for i in range(3))
                emb = ps[0:TOK, emb_at(t0):emb_at(t0) + n * 256].rearrange("p (t c) -> p t c", c=256)
                link(v.tensor_scalar(nm, emb[:, :, D], -1.0 / KD, None, ALU.mult))
                link(v.tensor_tensor(msq, nm, nm, ALU.mult))
                link(v.scalar_tensor_tensor(var, ps[0:TOK, ssq_at(t0):ssq_at(t0) + n], 1.0 / KD, msq, ALU.mult, ALU.subtract))
                rsqrt(var, t0, t1)
                for t in range(t0, t1):
                    last = v.scalar_tensor_tensor(y0[0:TOK, t, :], c1[0:TOK, :], small[0:TOK, 0, t:t + 1], emb[:, t - t0, 0:D], ALU.mult, ALU.add)
                link(last)
                for t in range(t0, t1):
                    last = v.scalar_tensor_tensor(y1[0:TOK, t, :], y0[0:TOK, t, :], rs[0:TOK, 0, t:t + 1], c2[0:TOK, :], ALU.mult, ALU.add)
                link(last)
                link(normalize(lambda t: y0[0:TOK, t, :], lambda t: y1[0:TOK, t, :], t0, t1))
                row = lambda w: spread(w[0:TOK, :].rearrange("p (o d) -> p o d", o=1), 1, n)
                link(v.tensor_tensor(y1[0:TOK, t0:t1, :], y0[0:TOK, t0:t1, :], row(ln2g_b), ALU.mult))
                link(v.tensor_tensor(h0[0:TOK, t0:t1, :], y1[0:TOK, t0:t1, :], row(ln2b_b), ALU.add))
                link(normalize(lambda t: y0[0:TOK, t, 0:Q], lambda t: h0[0:TOK, t, :], t0, t1))
                reduce_angle(y0[0:TOK, t0:t1, 0:Q], lambda i: ang[0:TOK, i, 0:n, :])
                dve.wait_ge(cos_ready, g + 2)
                qg = qx[0:TOK, t0:t1, :, 0:DK]
                v.tensor_tensor(qg, ang[0:TOK, 1, 0:n, :].rearrange("p t (h d) -> p t h d", d=DK),
                                spread(ctheta[0:TOK, :].rearrange("p (o h d) -> p o h d", o=1, d=DK), 1, n), ALU.mult).then_inc(q_ready, 1)
                dve.wait_ge(q_ready, g + 1)
                if g:
                    dve.wait_ge(qT_done, t0)
                link(v.tensor_copy(qh[0:TOK, 0, 0:n, :].rearrange("p t (h d) -> p t h d", d=DK), qg))
                v.tensor_tensor(qh[0:TOK, 1, 0:n, :].rearrange("p t (h d) -> p t h d", d=DK), qg,
                                qh[0:TOK, 0, 0:n, :].rearrange("p t (h d) -> p t h d", d=DK), ALU.subtract).then_inc(qhl_ready, 1)
                dve.wait_ge(qhl_ready, g + 1)
                for t in range(n):
                    for side in range(2):
                        for part_n in range(2):
                            src = spread(qh[0:TOK, part_n, t, :].rearrange("p (h o d) -> p h o d", o=1, d=DK), 2, 2)
                            dst = qab[0:TOK, t, side]
                            dst = dst[:, :, part_n:4:2, :] if side == 0 else dst[:, :, 2 * part_n:2 * part_n + 2, :]
                            last = v.tensor_copy(dst, src)
                    last.then_inc(qab_ready, 1)

            def middle(g):
                t0, t1 = GROUPS[g]
                n = t1 - t0
                dve.wait_ge(pv_done, t1)
                pv = pcol(2 * g, 0, n * HEADS * DX, TOK).rearrange("p (h d) -> p h d", d=DX)
                rd = rden[0:TOK, 0:n, :].rearrange("p t h -> p (t h)")
                link(v.reciprocal(rd, pv[:, :, DK]))
                v.tensor_tensor(o[0:TOK, 0:n, :].rearrange("p t (h d) -> p (t h) d", d=DK), pv[:, :, 0:DK],
                                spread(rd.rearrange("p (h o) -> p h o", o=1), 2, DK), ALU.mult).then_inc(o_ready, 1)
                dve.wait_ge(proj_done, g + 1)
                link(v.tensor_tensor(h1[0:TOK, t0:t1, :], h0[0:TOK, t0:t1, :],
                                     ps[0:TOK, 3 * BANK:3 * BANK + n * 256].rearrange("p (t c) -> p t c", c=256)[:, :, 0:D], ALU.add))
                normalize(lambda t: xs[0:TOK, t, 0, 0:D], lambda t: h1[0:TOK, t, :], t0, t1).then_inc(xn_ready, 1)

            def choose(g):
                t0, t1 = GROUPS[g]
                n = t1 - t0
                dve.wait_ge(logits_done, g + 1)
                v.tensor_copy(logit[0:TOK, t0:t1, :], pcol(7, 0, n * E, TOK).rearrange("p (t e) -> p t e", e=E)).then_inc(logits_read, 1)
                dve.wait_ge(logits_read, g + 1)
                for t in range(t0, t1):
                    last = v.max(top[0:TOK, t, :], logit[0:TOK, t, :])
                link(last)
                for t in range(t0, t1):
                    last = v.max_index(topi[0:TOK, t, :], top[0:TOK, t, :], logit[0:TOK, t, :])
                link(last)
                link(v.tensor_copy(topf[0:TOK, t0:t1, :], topi[0:TOK, t0:t1, :]))

            front(0)
            for n in range(6, 9):
                low_part(n)
            for n in range(9, 12):
                low_part(n)
            middle(0)
            choose(0)
            for n in range(12, 16):
                low_part(n)
            front(1)
            for n in range(16, 20):
                low_part(n)
            middle(1)
            choose(1)
            v.tensor_tensor(gap[:, :], top[:, :, 1], top[:, :, 0], ALU.subtract).then_inc(gap_ready, 1)
            eb = spread(e_iota[:, :].rearrange("p (o e) -> p o e", o=1), 1, TILES)
            vb = spread(valid[:, :].rearrange("p (t o) -> p t o", o=1), 2, E)
            v.tensor_tensor(hot[:, 0], eb, spread(topf[:, :, 0:1], 2, E), ALU.is_equal)
            link(v.tensor_tensor(hot[:, 1], eb, spread(topf[:, :, 1:2], 2, E), ALU.is_equal))
            link(v.tensor_tensor(posm[:, 0], hot[:, 0], hot[:, 1], ALU.add))
            v.tensor_tensor(either[:, 0:TILES, :], posm[:, 0], vb, ALU.mult).then_inc(either_ready, 1)
            dve.wait_ge(ranks_done, 1)
            te = TILES * E
            link(v.tensor_copy(place[:, :, :].rearrange("p t e -> p (t e)"), pcol(6, 0, te + E)))
            link(v.tensor_tensor(full[:, :, :], spread(place[:, TILES, :].rearrange("p (e o) -> p e o", o=1), 2, TILES), m_iota[:, :, :], ALU.is_gt))
            link(v.tensor_reduce(nch[:, 0, :], full[:, :, :], AX, ALU.add))
            link(v.tensor_tensor_scan(nch[:, 1, :], ones[:, 0:E], nch[:, 0, :], 0.0, ALU.mult, ALU.add))
            ends = nch[:, 1, :]
            link(v.tensor_tensor(base[:, :], ends, nch[:, 0, :], ALU.subtract))
            link(v.scalar_tensor_tensor(place[:, 0:TILES, :], spread(base[:, :].rearrange("p (o e) -> p o e", o=1), 1, TILES),
                                        float(CHUNK), place[:, 0:TILES, :], ALU.mult, ALU.add))
            for k in range(2):
                last = v.tensor_tensor(posm[:, k], hot[:, k], place[:, 0:TILES, :], ALU.mult)
            link(last)
            link(v.tensor_reduce(posf[:, :, :], posm[:, :, :, :], AX, ALU.add))
            v.tensor_copy(posi[:, :, :], posf[:, :, :]).then_inc(pos_ready, 1)
            link(v.tensor_tensor(cmp[:, :, :], c_iota[:, :, :], spread(ends.rearrange("p (o e) -> p o e", o=1), 1, CHUNKS), ALU.is_ge))
            link(v.tensor_reduce(cexp[:, :, :].rearrange("p a c -> p (a c)"), cmp[:, :, :], AX, ALU.add))
            link(v.scalar_tensor_tensor(cexp[:, :, :], cexp[:, :, :], float(E - 1), pow8[:, :, :], ALU.min, ALU.mult))
            link(v.tensor_reduce(words[:, :], cexp[:, :, :], AX, ALU.add))
            v.tensor_copy(wordsi[:, :], words[:, :]).then_inc(words_ready, 1)
            dve.wait_ge(gexp_ready, 1)
            link(v.tensor_scalar(wsel[:, 2, :], gexp[:, :], 1.0, None, ALU.add))
            link(v.reciprocal(wsel[:, 0, :], wsel[:, 2, :]))
            link(v.tensor_tensor(wsel[:, 1, :], wsel[:, 0, :], gexp[:, :], ALU.mult))
            for n in range(20, NP * E):
                low_part(n)

            def gate(n, s):
                dve.wait_ge(act_ready, n + 1)
                if not (isinstance(n, int) and n < 2):
                    dve.wait_ge(hidT_done, n - 1)
                v.tensor_tensor(hid[:, s % 2, :], act[:, s % 2, :], pcol(s % 3, BLK, BLK), ALU.mult).then_inc(hid_ready, 1)

            def hidden_low(n, s):
                dve.wait_ge(hh_ready, n + 1)
                v.tensor_tensor(hl[:, s % 2], pcol(4 + s % 2, 0, BLK).rearrange("p (h t) -> p h t", h=HT), hh[:, s % 2],
                                ALU.subtract).then_inc(hidT_ready, 1)

            def rows_low(c, j):
                dve.wait_ge(xh_ready, c + 1)
                v.tensor_tensor(x1l[:, j % 2, :], pcol(7, 0, CHUNK), x1h[:, j % 2, 0, :], ALU.subtract)
                v.tensor_tensor(x1h[D2:P, j % 2, 1, :], ps[D2:P, 7 * BANK + CHUNK:7 * BANK + 2 * CHUNK], x1h[D2:P, j % 2, 1, :],
                                ALU.subtract).then_inc(xcT_ready, 1)

            def finish(c, j, reuse):
                dve.wait_ge(down_done, c + 1)
                if reuse:
                    dve.wait_ge(y_out[j % 2], 8 * (c - j) + 16 * (j // 2))
                v.tensor_copy(yc[:, j % 2, :], pcol(Y_BANKS[j % 2], 0, D)).then_inc(y_ready, 1)

            def round4(first, last, c0, n0):
                for s in range(4 * STEPS):
                    j, r = divmod(s, STEPS)
                    gate(n0 + s, s)
                    if not (first and s == 0):
                        hidden_low(n0 + (s - 1), s - 1)
                    if r == 1 and not (last and j == 3):
                        rows_low(c0 + (j + 1), j + 1)
                    if r == 2 and not (first and j == 0):
                        if j == 0:
                            dve.wait_ge(down_done, c0)
                            dve.wait_ge(y_out[1], 8 * c0 - 16)
                            v.tensor_copy(yc[:, 1, :], pcol(Y_BANKS[1], 0, D)).then_inc(y_ready, 1)
                        else:
                            finish(c0 + (j - 1), j - 1, not (first and j - 1 < 2))

            rows_low(0, 0)
            round4(True, False, 0, 0)
            with dve.Fori(1, CHUNKS // 4 - 1) as i:
                round4(False, False, 4 * i, i * (4 * STEPS))
            round4(False, True, CHUNKS - 4, (CHUNKS - 4) * STEPS)
            hidden_low(CHUNKS * STEPS - 1, CHUNKS * STEPS - 1)
            finish(CHUNKS - 1, 3, True)
            dve.wait_ge(got_in, 64)
            for t in range(TILES):
                rows = TOK if t < TILES - 1 else LAST
                last = v.scalar_tensor_tensor(h1[0:rows, t, :], got[0:rows, 0, t, :], wsel[0:rows, 0, t:t + 1], h1[0:rows, t, :], ALU.mult, ALU.add)
            link(last)
            for t in range(TILES):
                rows = TOK if t < TILES - 1 else LAST
                v.scalar_tensor_tensor(h0[0:rows, t, :], got[0:rows, 1, t, :], wsel[0:rows, 1, t:t + 1], h1[0:rows, t, :], ALU.mult, ALU.add).then_inc(res_ready, 1)

        @block.tensor
        def _(pe):
            mm = nc.tensor.matmul
            tr = nc.tensor.transpose

            def embed(t, k0, k1):
                dst = ps[0:TOK, emb_at(t):emb_at(t) + D + 1]
                for k in range(k0, k1):
                    if k % KC == 0 and (t == 0 or k == 0):
                        wait_x(pe, t, k // KC)
                        if t == 0:
                            pe.wait_ge(gw_ready, k // KC + 1)
                    last = mm(dst, xbuf[:, t % 2, k, :], gw[:, k, :], start=k == 0, stop=k == KT - 1)
                if k1 == KT:
                    last.then_inc(tok_done, 1)

            def square_sum(t):
                pe.wait_ge(ssq_ready, t + 1)
                for i in range(2):
                    last = mm(ps[0:TOK, ssq_at(t):ssq_at(t) + 1], ssq[:, t % 2, i, :], ones[:, 0:1], start=i == 0, stop=i == 1)
                last.then_inc(ssq_done, 1)

            def turn_queries(t, i):
                pe.wait_ge(qab_ready, t + 1)
                if t >= 1:
                    pe.wait_ge(qT_ready, t)
                for side in range(2):
                    for a in range(HA):
                        j = side * HA + a
                        src = qab[0:TOK, i, side, a * HB:(a + 1) * HB].rearrange("p h r d -> p (h r d)")
                        last = tr(ps_qT[:, j * TP:j * TP + TOK], src, ident_h[0:TOK, 0:TOK])
                last.then_inc(qT_done, 1)

            def scores(t):
                pe.wait_ge(qT_ready, t + 1)
                for b in range(HB):
                    r = slice(32 * b, 32 * b + 32)
                    dst = ps[0:TOK, (3 + b) * BANK:(3 + b) * BANK + HA * TOK]
                    mm(dst, mask[r, 0, :], spread(mask[r, 1:2, :], 1, HA), start=True, stop=False)
                    for a in range(HA):
                        last = mm(dst[:, a * TOK:(a + 1) * TOK], qabT[r, a, 0:TOK], qabT[r, HA + a, 0:TOK], start=False, stop=a == HA - 1)
                last.then_inc(scores_done, 1)

            def weigh(t, i, g):
                pe.wait_ge(probs_ready, t + 1)
                for h in range(HEADS):
                    a, b = divmod(h, HB)
                    c = (2 * g) * BANK + (i * HEADS + h) * DX
                    last = mm(ps[0:TOK, c:c + DX], probs[0:TOK, b, a, :], qx[0:TOK, t, h, :], start=True, stop=True)
                last.then_inc(pv_done, 1)

            def project(g):
                t0, t1 = GROUPS[g]
                pe.wait_ge(o_ready, g + 1)
                for i in range(t1 - t0):
                    last = tr(pcol(1, i * TOK, TOK, Q), o[0:TOK, i, :], ident[0:TOK, 0:TOK])
                last.then_inc(oT_done, 1)
                pe.wait_ge(oT_ready, g + 1)
                for i in range(t1 - t0):
                    last = mm(ps[0:TOK, 3 * BANK + i * 256:3 * BANK + i * 256 + D], oT[:, i, :], wcomb[:, :], start=True, stop=True)
                last.then_inc(proj_done, 1)

            def turn_normed(g):
                t0, t1 = GROUPS[g]
                pe.wait_ge(xn_ready, g + 1)
                for i in range(t1 - t0):
                    tr(pcol(5, i * TOK, TOK), xs[0:TOK, t0 + i, 0, 0:P], ident[0:TOK, 0:TOK])
                    last = tr(pcol(6, i * TOK, TOK, D2), xs[0:TOK, t0 + i, 0, P:D], ident[0:TOK, 0:TOK])
                last.then_inc(xnT_done, 1)

            def route(g):
                t0, t1 = GROUPS[g]
                pe.wait_ge(xnT_ready, g + 1)
                for i in range(t1 - t0):
                    mm(pcol(7, i * E, E, TOK), xnT[:, 0, i, :], rt1[:, :], start=True, stop=False)
                    last = mm(pcol(7, i * E, E, TOK), xnT[0:D2, 1, i, :], rt2[:, :], start=False, stop=True)
                last.then_inc(logits_done, 1)

            embed(0, 0, KT)
            for t in range(1, 4):
                embed(t, 0, KT // 2)
                square_sum(t - 1)
                embed(t, KT // 2, KT)
                if t == 2:
                    pe.wait_ge(csum_ready, 1)
                    mm(pcol(6, 0, 2 * D), ones[:, :], csum.rearrange("p a d -> p (a d)"), start=True, stop=True).then_inc(c_bcast, 1)
            CUT = [0, 4, 8, 12, 16, 20, 24, 28, 32]
            pe.wait_ge(vec_consts, 1)
            pe.wait_ge(consts_in, N_CONSTS)
            for t in range(3):
                turn_queries(t, t)
                embed(4, CUT[2 * t], CUT[2 * t + 1])
                scores(t)
                if t == 0:
                    square_sum(3)
                embed(4, CUT[2 * t + 1], CUT[2 * t + 2])
                weigh(t, t, 0)
            embed(4, CUT[6], CUT[7])
            project(0)
            embed(4, CUT[7], CUT[8])
            square_sum(4)
            turn_normed(0)
            route(0)
            for t in range(3, 5):
                if t == 3:
                    pe.wait_ge(logits_read, 1)
                turn_queries(t, t - 3)
                scores(t)
                weigh(t, t - 3, 1)
            project(1)
            turn_normed(1)
            route(1)

            pe.wait_ge(either_ready, 1)
            mm(pcol(6, 0, (TILES + 1) * E), before[:, :], either[:, :, :].rearrange("p t e -> p (t e)"), start=True, stop=False)
            for t in range(TILES):
                last = mm(pcol(6, (t + 1) * E, (TILES - t) * E), ones_b[:, :], spread(either[:, t:t + 1, :], 1, TILES - t),
                          start=False, stop=t == TILES - 1)
            last.then_inc(ranks_done, 1)

            pe.wait_ge(words_ready, 1)
            word = [pe.alloc_register(f"chunk_word{k}") for k in range(2)]
            offs = [pe.alloc_register(f"expert_off{k}") for k in range(2)]
            TOP = 8 ** (CHUNKS // 2) - 1
            for k in range(2):
                pe.reg_mov(word[k], pe.value_load(wordsi[0:1, k:k + 1], min_val=0, max_val=TOP))

            def turn_rows(c, j):
                pe.wait_ge(xc_in[j % 4], 4 * (c - j % 4) + 16)
                if not (isinstance(c, int) and c == 0):
                    pe.wait_ge(xcT_ready, c)
                tr(pcol(7, 0, CHUNK), xc[:, j % 4, 0:P], ident[:, :])
                tr(pcol(7, CHUNK, CHUNK), xc[:, j % 4, P:P + CHUNK], ident[:, :]).then_inc(xcT_done, 1)

            def part_w(which, off, col, n):
                return (hi_w if which == 0 else lo_w)[:, bass.ds(off + (which * EW + col), n)]

            def gate_up(n, s, off):
                if not (isinstance(n, int) and n < 3):
                    pe.wait_ge(hid_ready, n - 2)
                j, r = divmod(s, STEPS)
                dst = pcol(s % 3, 0, 2 * BLK)
                k1, k2 = 2 * BLK * r, W2 + 2 * BLK * r
                mm(dst, x1h[:, j % 2, 0, :], part_w(0, off, k1, 2 * BLK), start=True, stop=False)
                mm(dst, x1h[:, j % 2, 0, :], part_w(1, off, k1, 2 * BLK), start=False, stop=False)
                mm(dst, x1l[:, j % 2, :], part_w(0, off, k1, 2 * BLK), start=False, stop=False)
                mm(dst, x1h[:, j % 2, 1, :], part_w(0, off, k2, 2 * BLK), start=False, stop=False)
                mm(dst, x1h[:, j % 2, 1, :], part_w(1, off, k2, 2 * BLK), start=False, stop=True).then_inc(gu_done, 1)

            def turn_hidden(n, s):
                pe.wait_ge(hid_ready, n + 1)
                if not (isinstance(n, int) and n < 2):
                    pe.wait_ge(hidT_ready, n - 1)
                for h in range(HT):
                    last = tr(pcol(4 + s % 2, h * P, P), hid[:, s % 2, h * P:(h + 1) * P], ident[:, :])
                last.then_inc(hidT_done, 1)

            def down(c, n, s, off):
                y = pcol(Y_BANKS[s // STEPS % 2], 0, D)
                pe.wait_ge(hidT_ready, n + 1)
                r = s % STEPS
                if r == 0 and not (isinstance(c, int) and c < 2):
                    pe.wait_ge(y_ready, c - 1)
                for h in range(HT):
                    k = r * HT + h
                    col = 2 * W2 + k * D
                    end = k == STEPS * HT - 1
                    mm(y, hh[:, s % 2, h, :], part_w(0, off, col, D), start=k == 0, stop=False)
                    mm(y, hh[:, s % 2, h, :], part_w(1, off, col, D), start=False, stop=False)
                    last = mm(y, hl[:, s % 2, h, :], part_w(0, off, col, D), start=False, stop=end)
                if r == STEPS - 1:
                    last.then_inc(down_done, 1)

            def offset(k):
                return pe.snap(offs[k], min_val=0, max_val=(E - 1) * 2 * EW)

            def round4(first, last, c0, n0):
                for s in range(4 * STEPS):
                    j, r = divmod(s, STEPS)
                    if r == 0:
                        w0 = pe.snap(word[0], min_val=0, max_val=TOP)
                        pe.reg_mov(offs[j % 2], ((w0 >> (3 * j)) & 7) * (2 * EW))
                    off = offset(j % 2)
                    if r == 0:
                        pe.wait_ge(xcT_ready, c0 + (j + 1))
                    gate_up(n0 + s, s, off)
                    if not (first and s < 1):
                        turn_hidden(n0 + (s - 1), s - 1)
                    if r == 1 and not (last and j == 3):
                        turn_rows(c0 + (j + 1), j + 1)
                    if not (first and s < 2):
                        jd = (s - 2) // STEPS
                        down(c0 + jd, n0 + (s - 2), s - 2, offset(jd % 2))
                w0 = pe.snap(word[0], min_val=0, max_val=TOP)
                w1 = pe.snap(word[1], min_val=0, max_val=TOP)
                pe.reg_mov(word[0], (w0 >> 12) | ((w1 & 4095) << 12))
                pe.reg_mov(word[1], w1 >> 12)

            turn_rows(0, 0)
            pe.wait_ge(split_done, NP * E)
            round4(True, False, 0, 0)
            with pe.Fori(1, CHUNKS // 4 - 1) as i:
                round4(False, False, 4 * i, i * (4 * STEPS))
            round4(False, True, CHUNKS - 4, (CHUNKS - 4) * STEPS)
            S = CHUNKS * STEPS
            down(CHUNKS - 1, S - 2, S - 2, offset(1))
            turn_hidden(S - 1, S - 1)
            down(CHUNKS - 1, S - 1, S - 1, offset(1))


def kernel(x, L0_tok_ln1_g, L0_tok_ln1_b, L0_tok_W_proj, L0_tok_b_proj, L0_tok_ln2_g, L0_tok_ln2_b,
           L0_attn_theta, L0_attn_W_combine, L0_ffn_router_w, L0_ffn_Wg, L0_ffn_Wu, L0_ffn_Wd):
    import numpy as np
    import concourse.bacc as bacc
    from concourse.bass_utils import run_bass_kernel_spmd

    P, PATCH, SEQ, IMGS, TILES, BLK = 128, 32, 9, 13, 5, 256
    x = np.asarray(x)
    B, C, H, W = x.shape
    tok = x.reshape(B, C, H // PATCH, PATCH, W // PATCH, PATCH).transpose(0, 2, 4, 3, 5, 1).reshape(B * SEQ, -1)
    K = tok.shape[1]
    KT = K // P
    TOK = IMGS * SEQ
    full = np.zeros((TILES * TOK, K), tok.dtype)
    full[:B * SEQ] = tok
    xt = full.reshape(TILES, TOK, P, KT).transpose(0, 2, 3, 1)
    Wg, Wu, Wd = (np.asarray(a) for a in (L0_ffn_Wg, L0_ffn_Wu, L0_ffn_Wd))
    E, HID, D = Wg.shape
    gu = np.stack([Wg.transpose(0, 2, 1).reshape(E, D, HID // BLK, BLK),
                   Wu.transpose(0, 2, 1).reshape(E, D, HID // BLK, BLK)], axis=3).reshape(E, D, 2 * HID)
    wd = Wd.transpose(0, 2, 1).reshape(E, HID // P, P, D).transpose(0, 2, 1, 3).reshape(E, P, -1)
    w_exp = np.concatenate([gu[:, :P], np.concatenate([gu[:, P:], gu[:, P:]], axis=1), wd], axis=2)
    ins = {
        "x_t": xt,
        "ln1_g": np.asarray(L0_tok_ln1_g).reshape(P, KT), "ln1_b": np.asarray(L0_tok_ln1_b).reshape(P, KT),
        "w_proj": np.asarray(L0_tok_W_proj), "b_proj": np.asarray(L0_tok_b_proj),
        "ln2_g": np.asarray(L0_tok_ln2_g), "ln2_b": np.asarray(L0_tok_ln2_b),
        "theta": np.asarray(L0_attn_theta), "w_comb": np.asarray(L0_attn_W_combine).T,
        "router": np.asarray(L0_ffn_router_w).T, "w_exp": w_exp,
    }
    ins = {k: np.ascontiguousarray(a) for k, a in ins.items()}
    nc = bacc.Bacc("TRN2", target_bir_lowering=False, num_devices=1)
    args = [nc.dram_tensor(k, a.shape, mybir.dt.from_np(a.dtype), kind="ExternalInput").ap() for k, a in ins.items()]
    n_tok = B * SEQ
    chunks = (2 * n_tok + E * (P - 1)) // P
    args.append(nc.dram_tensor("out", (n_tok, D), mybir.dt.float32, kind="ExternalOutput").ap())
    args.append(nc.dram_tensor("slot_x", (chunks * P, 2 * P + 1), mybir.dt.float32, kind="Internal").ap())
    args.append(nc.dram_tensor("pair_y", (2 * n_tok + chunks * P, D), mybir.dt.float32, kind="Internal").ap())
    vit_tower(nc, *args)
    r = run_bass_kernel_spmd(nc, [ins], core_ids=[0])
    return r.results[0]["out"].reshape(B, SEQ, D)
```

```python
import math
from contextlib import ExitStack

import concourse.bass as bass
from concourse import mybir


def vit_tower(nc, x, ln1_g, ln1_b, w_proj, b_proj, ln2_g, ln2_b, theta, w_comb, router,
              w_exp, out, slot_x, pair_y):
    f32 = mybir.dt.float32
    f16 = mybir.dt.float16
    bf16 = mybir.dt.bfloat16
    i32 = mybir.dt.int32
    u32 = mybir.dt.uint32
    ALU = mybir.AluOpType
    ACT = mybir.ActivationFunctionType
    AX = mybir.AxisListType.X

    TILES, P, KT, TOKX = x.shape
    TOK = TOKX - 1
    ONE_Q = TOK // 32 * 32
    D = w_proj.shape[1]
    D2 = D - P
    KD = KT * P
    SEQ = 9
    IMGS = TOK // SEQ
    NTOK = out.shape[0]
    LAST = NTOK - (TILES - 1) * TOK
    Q = theta.shape[0]
    HEADS = 12
    DK = Q // HEADS
    HB = 4
    HA = HEADS // HB
    DX = DK + 1
    E, _, EW = w_exp.shape
    HID = 768
    W2 = 2 * HID
    BLK = 256
    STEPS = HID // BLK
    HT = BLK // P
    CHUNK = P
    CHUNKS = (2 * NTOK + E * (CHUNK - 1)) // CHUNK
    FIRST = 4
    ROW = D + (P - D2) + 1
    NP = 8
    PW = EW // NP
    STAGES = 7
    GROUPS = [(0, 2), (2, 4), (4, 5)]
    EPS = 1e-5
    BIG = 512.0
    MAGIC = 1.5 * 2.0 ** 23
    TWO_PI_A = 6.28125
    TWO_PI_B = 2 * math.pi - TWO_PI_A
    RSQRT_SEED = float(0x5F3759DF)
    EARLY = 4

    VEC_PIECES = (12, 13, 27, 32, 34, 35, 36, 43, 44, 51, 59, 61, 63)

    def on_pool(n):
        return n >= NP and n not in VEC_PIECES

    def splits(n):
        return sum(on_pool(i) == on_pool(n) for i in range(n + 1))

    def spread(ap, dim, n):
        shape = list(ap.shape)
        shape[dim] = n
        return ap.broadcast_to(shape)

    ctx = ExitStack()
    with ctx:
        def sb(name, shape, dt=f32):
            return ctx.enter_context(nc.sbuf_tensor(name, shape, dt))

        def sem(name):
            return ctx.enter_context(nc.semaphore(name))

        experts = sb("experts", [P, E * EW])
        flat = experts[:, :]
        hi_w = flat.bitcast(f16)
        lo_w = flat.bitcast(bf16)
        at = EARLY * EW
        gw = flat[:, at:at + KT * (D + 1)].rearrange("p (k d) -> p k d", k=KT)
        at += KT * (D + 1)
        xbuf = flat[:, at:at + 2 * KT * TOKX].rearrange("p (b k t) -> p b k t", b=2, k=KT)
        at += 2 * KT * TOKX
        GS = 4
        NG = KT // GS
        sq = flat[:, at:at + 2 * GS * TOK].rearrange("p (b k t) -> p b k t", b=2, k=GS)
        at += 2 * GS * TOK
        ssq = flat[:, at:at + 2 * GS * TOK].rearrange("p (b k t) -> p b k t", b=2, k=GS)
        at += 2 * GS * TOK

        def carve(size, dt=f32):
            nonlocal at
            at += size
            assert at <= E * EW
            return flat[:, at - size:at].bitcast(dt)

        diff = carve(P, i32)
        part = carve(TOK, i32)
        imgd = carve(TOK, i32).rearrange("p (i r) -> p i r", i=IMGS)
        mask_f = carve(3 * TOK).rearrange("p (a t) -> p a t", a=3)
        blank = carve(ROW - 1)
        spare_pair = carve(CHUNKS, i32)
        theta_b = carve(Q)
        e_iota_i = carve(E, i32)
        c_iota_i = carve(CHUNKS * E, i32).rearrange("p (c e) -> p c e", e=E)
        m_iota_i = carve(E * TILES, i32).rearrange("p (e t) -> p e t", e=E)
        wraw = flat[:, 2 * EW:2 * EW + KT * D].rearrange("p (k d) -> p k d", k=KT)
        stage = sb("stage", [P, STAGES, PW])
        gcol = sb("gcol", [P, KT])
        bcol = sb("bcol", [P, KT])
        ones = sb("ones", [P, P])
        ones_b = sb("ones_b", [P, P], bf16)
        ident = sb("ident", [P, P])
        ident_h = sb("ident_h", [P, P], f16)
        before = sb("before", [P, P], bf16)
        mask = sb("mask", [P, 2, TOK], f16)
        e_iota = sb("e_iota", [P, E])
        c_iota = sb("c_iota", [P, CHUNKS, E])
        m_iota = sb("m_iota", [P, E, TILES])
        pow8 = sb("pow8", [P, 2, CHUNKS // 2])
        validi = sb("validi", [P, TILES], i32)
        valid = sb("valid", [P, TILES])
        ln2g_b = sb("ln2g_b", [P, D])
        ln2b_b = sb("ln2b_b", [P, D])
        bproj_b = sb("bproj_b", [P, D])
        wcomb = sb("wcomb", [Q, D])
        rt1 = sb("rt1", [P, E])
        rt2 = sb("rt2", [D2, E])
        halfpi = sb("halfpi", [P, 1])
        ctheta = sb("ctheta", [P, Q])
        c1 = sb("c1", [P, D])
        c2 = sb("c2", [P, D])
        small = sb("small", [P, 3, TILES])
        bns = sb("bns", [P, TILES, 6])
        mv = sb("mv", [P, TILES, 2])
        rs = sb("rs", [P, 3, TILES])
        rsi = sb("rsi", [P, TILES], i32)
        yy = sb("yy", [P, 2, TILES, D])[:, :, :, :]
        y0 = yy[:, 0]
        y1 = yy[:, 1]
        h0 = sb("h0", [P, TILES, D])
        h1 = sb("h1", [P, TILES, D])
        qx = sb("qx", [P, TILES, HEADS, DX])
        qh = sb("qh", [P, 2, 3, Q], f16)
        QAB = TILES * 2 * HEADS * 4 * DK // 2
        PRB = HB * HA * TOK
        ANG = 3 * 3 * Q
        shared = sb("shared", [P, QAB + PRB + ANG])
        qab = shared[:, 0:QAB].bitcast(f16).rearrange("p (t s h r d) -> p t s h r d", t=TILES, s=2, h=HEADS, r=4)
        probs = shared[:, QAB:QAB + PRB].rearrange("p (b a t) -> p b a t", b=HB, a=HA)
        csum = h1[:, 0, :]
        c1_row = h1[ONE_Q:TOKX, 1, :]
        pick_one = yy[ONE_Q:TOKX, 0, 0, 0:TOK]
        ang = shared[:, QAB + PRB:QAB + PRB + ANG].rearrange("p (i t q) -> p i t q", i=3, t=3)
        xnT = shared[:, QAB + PRB:QAB + PRB + 2 * 3 * TOK].rearrange("p (k t n) -> p k t n", k=2, t=3)
        TP = TOK + 1
        qabT = sb("qabT", [P, 2 * HA, TP], f16)
        rden = sb("rden", [P, 3, HEADS])
        o = sb("o", [P, 3, Q])
        oT = sb("oT", [Q, 3, TOK])
        xs = sb("xs", [P, TILES, 2, ROW])
        top = sb("top", [P, TILES, 8])
        logit = sb("logit", [P, TILES, E])
        topi = sb("topi", [P, TILES, 8], u32)
        topf = sb("topf", [P, TILES, 8])
        gap = sb("gap", [P, TILES])
        gexp = sb("gexp", [P, TILES])
        wsel = sb("wsel", [P, 3, TILES])
        hot = sb("hot", [P, 2, TILES, E])
        either = sb("either", [P, TILES + 1, E], bf16)
        place = sb("place", [P, TILES + 1, E])
        full = sb("full", [P, E, TILES])
        nch = sb("nch", [P, 3, E])
        base = sb("base", [P, E])
        posm = sb("posm", [P, 2, TILES, E])
        posf = sb("posf", [P, 2, TILES])
        posi = sb("posi", [P, 2, TILES], u32)
        cmp = sb("cmp", [P, CHUNKS, E])
        cexp = sb("cexp", [P, 2, CHUNKS // 2])
        words = sb("words", [P, 2])
        wordsi = sb("wordsi", [P, 2], i32)
        at2 = 0

        def reuse_shared(words, dt=f32):
            nonlocal at2
            at2 += words
            assert at2 <= QAB + PRB + ANG
            return shared[:, at2 - words:at2].bitcast(dt)

        xc = reuse_shared(4 * ROW).rearrange("p (j w) -> p j w", j=4)
        x1h = reuse_shared(2 * CHUNK, f16).rearrange("p (j k t) -> p j k t", j=2, k=2)
        x1l = reuse_shared(CHUNK, f16).rearrange("p (j t) -> p j t", j=2)
        act = reuse_shared(2 * BLK).rearrange("p (j n) -> p j n", j=2)
        hid = reuse_shared(2 * BLK).rearrange("p (j n) -> p j n", j=2)
        hh = reuse_shared(BLK, f16).rearrange("p (j h t) -> p j h t", j=2, h=HT)
        hl = reuse_shared(BLK, bf16).rearrange("p (j h t) -> p j h t", j=2, h=HT)
        yc = reuse_shared(2 * D).rearrange("p (j d) -> p j d", j=2)
        slot_iota = sb("slot_iota", [P, CHUNK])
        own = sb("own", [P, 1])
        posc = sb("posc", [P, FIRST, 2, TILES])
        PARTS = 2 * D
        late = yy.rearrange("p a t d -> p (a t d)").bitcast(f16)
        parts = late[:, 0:TILES * PARTS].rearrange("p (t c) -> p t c", t=TILES)
        picks = late[:, TILES * PARTS:TILES * (PARTS + 3 * CHUNK)].rearrange("p (b t c) -> p b t c", b=3, t=TILES)
        got = yy

        BANK = 512
        ps = ctx.enter_context(nc.psum_tensor("ps", [P, 8 * BANK], f32))

        def pcol(b, off, n, rows=P):
            return ps[0:rows, b * BANK + off:b * BANK + off + n]

        Y_BANKS = (3, 6)
        ps_qT = pcol(7, 0, BANK).bitcast(f16)

        def emb_at(t):
            return t * 256

        def ssq_at(t):
            return (7 * BANK + 400 if t < 2 else t // 2 * BANK + 500) + t

        def in_group(g, off, n, rows):
            return ps[0:rows, g * BANK + off:g * BANK + off + n]

        LOGITS = BANK - 2 * E

        w_in = [sem(f"w_in{j}") for j in range(4)]
        x0_in = [sem(f"x0_in{j}") for j in range(4)]
        x_in = [sem("x_in0"), sem("x_in1")]
        gain_in = sem("gain_in")
        bias_in = sem("bias_in")
        consts_in = sem("consts_in")
        stage_in = [sem(f"stage_in{j}") for j in range(STAGES)]
        hi_done = sem("hi_done")
        split_vec = sem("split_vec")
        split_pool = sem("split_pool")
        blank_out = sem("blank_out")
        pool_consts = sem("pool_consts")
        vec_consts = sem("vec_consts")
        gw_ready = sem("gw_ready")
        csum_ready = sem("csum_ready")
        c1_ready = sem("c1_ready")
        c_bcast = sem("c_bcast")
        sq_ready = sem("sq_ready")
        sq_used = sem("sq_used")
        ssq_ready = sem("ssq_ready")
        ssq_done = sem("ssq_done")
        tok_done = sem("tok_done")
        abs_ready = sem("abs_ready")
        cos_ready = sem("cos_ready")
        q_ready = sem("q_ready")
        qhl_ready = sem("qhl_ready")
        qab_ready = sem("qab_ready")
        qT_done = sem("qT_done")
        qT_ready = sem("qT_ready")
        scores_done = sem("scores_done")
        probs_ready = sem("probs_ready")
        pv_done = sem("pv_done")
        o_ready = sem("o_ready")
        oT_done = sem("oT_done")
        oT_ready = sem("oT_ready")
        proj_done = sem("proj_done")
        xn_ready = sem("xn_ready")
        xs_ready = sem("xs_ready")
        parts_high = sem("parts_high")
        parts_ready = sem("parts_ready")
        picks_ready = sem("picks_ready")
        xnT_done = sem("xnT_done")
        xnT_ready = sem("xnT_ready")
        logits_done = sem("logits_done")
        gap_ready = sem("gap_ready")
        gexp_ready = sem("gexp_ready")
        either_ready = sem("either_ready")
        ranks_done = sem("ranks_done")
        pos_ready = sem("pos_ready")
        words_ready = sem("words_ready")
        scattered = sem("scattered")
        xc_in = [sem(f"xc_in{j}") for j in range(4)]
        xcT_done = sem("xcT_done")
        xh_ready = sem("xh_ready")
        xcT_ready = sem("xcT_ready")
        gu_done = sem("gu_done")
        act_ready = sem("act_ready")
        hid_ready = sem("hid_ready")
        hidT_done = sem("hidT_done")
        hh_ready = sem("hh_ready")
        hidT_ready = sem("hidT_ready")
        down_done = sem("down_done")
        y_ready = sem("y_ready")
        y_out = [sem("y_out0"), sem("y_out1")]
        got_in = [sem("got_in0"), sem("got_in1")]
        res_ready = sem("res_ready")
        out_done = sem("out_done")
        vchain = sem("vchain")
        pchain = sem("pchain")

        N_CONSTS = 7 * 16
        KC = KT // 4

        def wait_x(eng, t, j):
            if t == 0:
                eng.wait_ge(x0_in[j], 16)
            else:
                eng.wait_ge(x_in[t % 2], 16 * ((t + 1) // 2))

        def take_rest(eng, ops, n):
            e, j = divmod(n, NP)
            to = 2 * e * EW + j * PW
            eng.wait_ge(hi_done, n + 1)
            ops.tensor_tensor(lo_w[:, to + EW:to + EW + PW], stage[:, n % STAGES, :], hi_w[:, to:to + PW],
                              ALU.subtract).then_inc(split_pool if on_pool(n) else split_vec, 1)

        block = ctx.enter_context(nc.Block())

        @block.sync
        def _(sp):
            def load_x(t):
                if t >= 2:
                    sp.wait_ge(tok_done, t - 1)
                    sp.wait_ge(sq_ready, NG * (t - 1))
                sp.dma_start(xbuf[:, t % 2], x[t]).then_inc(x_in[t % 2], 16)

            def load_piece(n):
                e, j = divmod(n, NP)
                k = n % STAGES
                if n >= STAGES:
                    sp.wait_ge(split_pool if on_pool(n - STAGES) else split_vec, splits(n - STAGES))
                sp.dma_start(stage[:, k, :], w_exp[e, :, j * PW:(j + 1) * PW]).then_inc(stage_in[k], 16)

            sp.dma_start(gcol[:, :], ln1_g).then_inc(gain_in, 16)
            wsrc = w_proj.rearrange("(p k) d -> p k d", p=P)
            for j in range(4):
                ks = slice(j * KC, (j + 1) * KC)
                sp.dma_start(wraw[:, ks, :], wsrc[:, ks, :]).then_inc(w_in[j], 16)
                sp.dma_start(xbuf[:, 0, ks, :], x[0, :, ks, :]).then_inc(x0_in[j], 16)
            sp.dma_start(bcol[:, :], ln1_b).then_inc(bias_in, 16)
            load_x(1)
            for dst, src in ((theta_b, theta), (ln2g_b, ln2_g), (ln2b_b, ln2_b), (bproj_b, b_proj)):
                sp.dma_start(dst[:, :], spread(src.rearrange("(o n) -> o n", o=1), 0, P)).then_inc(consts_in, 16)
            sp.dma_start(wcomb[:, :], w_comb).then_inc(consts_in, 16)
            sp.dma_start(rt1[:, :], router[0:P, :]).then_inc(consts_in, 16)
            sp.dma_start(rt2[:, :], router[P:D, :]).then_inc(consts_in, 16)
            for n in range(0, STAGES):
                load_piece(n)
            load_x(2)
            for n in range(STAGES, 9):
                load_piece(n)
            load_x(3)
            for n in range(9, 14):
                load_piece(n)
            load_x(4)
            sp.wait_ge(pool_consts, 1)
            slots = slot_x.rearrange("(c p) w -> p c w", p=CHUNK)
            sp.dma_start(slots[:, :, 0:ROW - 1], spread(blank[:, :].rearrange("p (o w) -> p o w", o=1), 1, CHUNKS)).then_inc(blank_out, 16)
            sp.dma_start(slots[:, :, ROW - 1:ROW].bitcast(i32), spare_pair[:, :].rearrange("p (c o) -> p c o", o=1),
                         allow_slow_non_contiguous=True).then_inc(blank_out, 16)
            for n in range(14, NP * E):
                load_piece(n)

            sp.wait_ge(scattered, 16 * 2 * TILES)

            def load_chunk(c, j, reuse):
                if reuse:
                    sp.wait_ge(y_out[j % 2], 8 * (c - j) + (16 * (j // 2) - 16))
                sp.dma_start(xc[:, j, :], slot_x[bass.ts(c, CHUNK), :]).then_inc(xc_in[j], 16)

            for j in range(4):
                load_chunk(j, j, False)
            with sp.Fori(1, CHUNKS // 4) as i:
                for j in range(4):
                    load_chunk(4 * i + j, j, True)
            for k in range(2):
                sp.wait_ge(y_out[k], 16 * (CHUNKS // 2))
            for k in range(2):
                for a, n, rows in ((0, TILES - 1, TOK), (TILES - 1, 1, LAST)):
                    r0 = k * NTOK + a * TOK
                    sp.dma_start(got[0:rows, k, a:a + n, :],
                                 pair_y[r0:r0 + n * rows, :].rearrange("(t p) d -> p t d", p=rows)).then_inc(got_in[k], 16)
            STORES = ((0, 2, TOK), (2, TILES - 3, TOK), (TILES - 1, 1, LAST))
            for a, n, rows in STORES:
                sp.wait_ge(res_ready, a + n)
                sp.dma_start(out[a * TOK:a * TOK + n * rows, :].rearrange("(t p) d -> p t d", p=rows),
                             h0[0:rows, a:a + n, :]).then_inc(out_done, 16)
            sp.wait_ge(out_done, 16 * len(STORES))

        @block.gpsimd
        def _(pool):
            steps = [0]

            def link(ins):
                steps[0] += 1
                ins.then_inc(pchain, 1)
                pool.wait_ge(pchain, steps[0])

            g = nc.gpsimd
            g.memset(ones[:, :], 1.0)
            g.memset(halfpi[:, :], math.pi / 2)
            g.memset(blank[:, :], 0.0)
            g.memset(ones_b[:, :], 1.0)
            g.memset(qx[:, :, :, :], 1.0)
            for c in range(CHUNKS // 2):
                g.memset(pow8[:, :, c:c + 1], 8.0 ** c)
            link(g.iota(diff[:, :], pattern=[[-1, P]], base=0, channel_multiplier=1))
            for b in range(HB):
                r = slice(32 * b, 32 * b + 32)
                link(g.iota(part[r, :], pattern=[[0, TOK]], base=0, channel_multiplier=1))
                link(g.iota(imgd[r, :, :], pattern=[[1, IMGS], [0, SEQ]], base=0, channel_multiplier=-1))
            g.iota(e_iota_i[:, :], pattern=[[1, E]], base=0, channel_multiplier=0)
            g.iota(c_iota_i[:, :, :], pattern=[[1, CHUNKS], [0, E]], base=0, channel_multiplier=0)
            g.iota(m_iota_i[:, :, :], pattern=[[0, E], [CHUNK, TILES]], base=0, channel_multiplier=0)
            for t in range(TILES):
                for k in range(2):
                    g.iota(xs[:, t, k, ROW - 1:ROW].bitcast(i32), pattern=[[0, 1]], base=k * NTOK + t * TOK, channel_multiplier=1)
            g.iota(validi[:, :], pattern=[[TOK, TILES]], base=0, channel_multiplier=1)
            g.iota(spare_pair[:, :], pattern=[[CHUNK, CHUNKS]], base=2 * NTOK, channel_multiplier=1).then_inc(pool_consts, 1)
            for t in range(TILES):
                acc = ssq[:, t % 2]
                for j in range(1, NG):
                    n = NG * t + j
                    pool.wait_ge(sq_ready, n + 1)
                    added = (NG - 1) * t + j
                    g.tensor_tensor(acc, acc, sq[:, added % 2], ALU.add).then_inc(sq_used, 1)
                    pool.wait_ge(sq_used, added)
                g.tensor_tensor(acc[:, 0:2], acc[:, 0:2], acc[:, 2:4], ALU.add).then_inc(ssq_ready, 1)
            for n in range(NP * E):
                if on_pool(n):
                    take_rest(pool, g, n)
            pool.wait_ge(blank_out, 32)
            pool.wait_ge(xs_ready, len(GROUPS))
            pool.wait_ge(pos_ready, 1)
            for t in range(TILES):
                rows = TOK if t < TILES - 1 else LAST
                for k in range(2):
                    pool.indirect_dma_start(
                        out=slot_x, out_offset=bass.IndirectOffsetOnAxis(ap=posi[0:rows, k, t:t + 1], axis=0),
                        in_=xs[0:rows, t, k, :], in_offset=None).then_inc(scattered, 16)

            for c in range(CHUNKS):
                pool.wait_ge(xc_in[c % 4], 16 * (c // 4 + 1))
                pool.wait_ge(y_ready, c + 1)
                pool.indirect_dma_start(
                    out=pair_y, out_offset=bass.IndirectOffsetOnAxis(ap=xc[:, c % 4, ROW - 1:ROW].bitcast(u32), axis=0),
                    in_=yc[:, c % 2, :], in_offset=None).then_inc(y_out[c % 2], 16)

        @block.scalar
        def _(sc):
            a = nc.scalar

            def squares(t, j0, j1):
                for j in range(j0, j1):
                    n = NG * t + j
                    wait_x(sc, t, j * GS // KC)
                    if j == 0 and t >= 2:
                        sc.wait_ge(ssq_done, t - 1)
                    if j > 0 and (NG - 1) * t + j > 2:
                        sc.wait_ge(sq_used, (NG - 1) * t + j - 2)
                    dst = ssq[:, t % 2] if j == 0 else sq[:, ((NG - 1) * t + j) % 2]
                    a.activation(dst, xbuf[:, t % 2, j * GS:(j + 1) * GS, 0:TOK], ACT.Square).then_inc(sq_ready, 1)

            def high_part(n):
                e, j = divmod(n, NP)
                to = 2 * e * EW + j * PW
                if n == NP * 2:
                    sc.wait_ge(csum_ready, 1)
                if n == NP * EARLY:
                    sc.wait_ge(tok_done, TILES)
                    sc.wait_ge(ssq_done, TILES)
                    sc.wait_ge(blank_out, 32)
                sc.wait_ge(stage_in[n % STAGES], 16 * (n // STAGES + 1))
                a.copy(hi_w[:, to:to + PW], stage[:, n % STAGES, :]).then_inc(hi_done, 1)

            def cosine(n, dst, src):
                sc.wait_ge(abs_ready, n + 1)
                a.activation(dst, src, ACT.Sin, bias=halfpi[0:TOK, 0:1], scale=-1.0).then_inc(cos_ready, 1)

            def turned(t):
                sc.wait_ge(qT_done, t + 1)
                a.copy(qabT[:, :, 0:TOK], ps_qT[:, 0:2 * HA * TP].rearrange("p (g t) -> p g t", t=TP)[:, :, 0:TOK]).then_inc(qT_ready, 1)

            def attend(t):
                sc.wait_ge(scores_done, t + 1)
                if t >= 1:
                    sc.wait_ge(pv_done, t)
                a.activation(probs[0:TOK].rearrange("p b a t -> p b (a t)"),
                             ps[0:TOK, 3 * BANK:7 * BANK].rearrange("p (b n) -> p b n", b=HB)[:, :, 0:HA * TOK],
                             ACT.Exp, scale=DK ** -0.5).then_inc(probs_ready, 1)

            def outputs(g):
                t0, t1 = GROUPS[g]
                n = t1 - t0
                sc.wait_ge(oT_done, g + 1)
                if g:
                    sc.wait_ge(proj_done, g)
                a.copy(oT[:, 0:n, :], in_group(g, 0, n * TOK, Q).rearrange("p (t c) -> p t c", t=n)).then_inc(oT_ready, 1)

            def rows(g):
                t0, t1 = GROUPS[g]
                n = t1 - t0
                sc.wait_ge(xn_ready, g + 1)
                sc.wait_ge(xnT_done, g + 1)
                if g:
                    sc.wait_ge(logits_done, g)
                a.copy(xnT[:, 0, 0:n, :], in_group(g, 0, n * TOK, P).rearrange("p (t c) -> p t c", t=n))
                a.copy(xnT[0:D2, 1, 0:n, :], in_group(g, 2 * TOK, n * TOK, D2).rearrange("p (t c) -> p t c", t=n)).then_inc(xnT_ready, 1)
                a.copy(parts[0:TOK, t0:t1, 0:D], xs[0:TOK, t0:t1, 0, 0:D]).then_inc(parts_high, 1)

            def both_choices(g):
                t0, t1 = GROUPS[g]
                for k in range(2):
                    if k:
                        a.copy(xs[0:TOK, t0:t1, k, 0:D], xs[0:TOK, t0:t1, 0, 0:D])
                    last = a.copy(xs[0:TOK, t0:t1, k, D:ROW - 1], xs[0:TOK, t0:t1, 0, P:D])
                last.then_inc(xs_ready, 1)

            def high_parts(n0, n1):
                for n in range(n0, n1):
                    high_part(n)

            sc.wait_ge(pool_consts, 1)
            squares(0, 0, NG)
            squares(1, 0, NG // 2)
            for j in range(4):
                squares(1, 4 + j, 5 + j)
                high_part(j)
            for j in range(NG):
                squares(2, j, j + 1)
                if j == 2:
                    sc.wait_ge(tok_done, 2)
                    a.copy(c1_row, ps[ONE_Q:TOKX, emb_at(0):emb_at(0) + D]).then_inc(c1_ready, 1)
                if j in (0, 1, 5, 6, 7):
                    high_part(4 + j - (3 if j > 1 else 0))
            cosine(0, ctheta[0:TOK, :], ang[0:TOK, 0, 0, :])
            for j in range(NG):
                squares(3, j, j + 1)
                if j > 2:
                    high_part(6 + j)
            cosine(1, ang[0:TOK, 1, 0:2], ang[0:TOK, 0, 0:2])
            squares(4, 0, 3)
            turned(0)
            squares(4, 3, 5)
            attend(0)
            turned(1)
            squares(4, 5, NG)
            attend(1)
            cosine(2, ang[0:TOK, 1, 0:2], ang[0:TOK, 0, 0:2])
            high_parts(14, 21)
            turned(2)
            high_parts(21, 22)
            attend(2)
            turned(3)
            high_parts(22, 29)
            cosine(3, ang[0:TOK, 1, 0:1], ang[0:TOK, 0, 0:1])
            outputs(0)
            high_parts(29, 30)
            attend(3)
            turned(4)
            high_parts(30, 38)
            outputs(1)
            attend(4)
            high_parts(38, 47)
            outputs(2)
            rows(0)
            high_parts(47, 49)
            rows(1)
            high_parts(49, 52)
            rows(2)
            high_parts(52, 57)
            sc.wait_ge(gap_ready, 1)
            a.activation(gexp[:, :], gap[:, :], ACT.Exp).then_inc(gexp_ready, 1)
            high_parts(57, 61)
            both_choices(0)
            high_parts(61, 63)
            both_choices(1)
            high_parts(63, NP * E)
            both_choices(2)

            def silu(n, s):
                sc.wait_ge(gu_done, n + 1)
                if not (isinstance(n, int) and n < 2):
                    sc.wait_ge(hid_ready, n - 1)
                a.activation(act[:, s % 2, :], pcol(s % 3, 0, BLK), ACT.Silu).then_inc(act_ready, 1)

            def hidden_high(n, s):
                sc.wait_ge(hidT_done, n + 1)
                a.copy(hh[:, s % 2], pcol(4 + s % 2, 0, BLK).rearrange("p (h t) -> p h t", h=HT)).then_inc(hh_ready, 1)

            def rows_picked(c):
                sc.wait_ge(xcT_done, c + 1)
                a.copy(x1h[:, c % 2], pcol(7, 0, 2 * CHUNK).rearrange("p (k t) -> p k t", k=2)).then_inc(xh_ready, 1)
                a.copy(x1l[:, c % 2, :], pcol(7, 2 * CHUNK, CHUNK)).then_inc(xcT_ready, 1)

            def rows_high(c, j):
                if isinstance(c, int) and c < FIRST:
                    return rows_picked(c)
                sc.wait_ge(xcT_done, c + 1)
                a.copy(x1h[:, j % 2], pcol(7, 0, 2 * CHUNK).rearrange("p (k t) -> p k t", k=2)).then_inc(xh_ready, 1)

            def round4(first, last, c0, n0):
                for s in range(4 * STEPS):
                    j, r = divmod(s, STEPS)
                    silu(n0 + s, s)
                    if not (first and s == 0):
                        hidden_high(n0 + (s - 1), s - 1)
                    if r == 1 and not (last and j == 3):
                        rows_high(c0 + (j + 1), j + 1)

            rows_high(0, 0)
            round4(True, False, 0, 0)
            with sc.Fori(1, CHUNKS // 4 - 1) as i:
                round4(False, False, 4 * i, i * (4 * STEPS))
            round4(False, True, CHUNKS - 4, (CHUNKS - 4) * STEPS)
            hidden_high(CHUNKS * STEPS - 1, CHUNKS * STEPS - 1)

        @block.vector
        def _(dve):
            v = nc.vector
            steps = [0]

            def link(ins):
                steps[0] += 1
                ins.then_inc(vchain, 1)
                dve.wait_ge(vchain, steps[0])

            def rests(n0, n1):
                for n in range(n0, n1):
                    if not on_pool(n):
                        take_rest(dve, v, n)

            def rsqrt(var, t0, t1):
                vv, y, w = (rs[0:TOK, i, t0:t1] for i in (1, 0, 2))
                link(v.tensor_scalar(vv, var, 1.0, EPS, ALU.mult, ALU.add))
                link(v.tensor_scalar(rsi[0:TOK, t0:t1], vv.bitcast(i32), -0.5, RSQRT_SEED, ALU.mult, ALU.add))
                at = rsi[0:TOK, t0:t1].bitcast(f32)
                for _ in range(3):
                    link(v.scalar_tensor_tensor(w, at, -0.5, at, ALU.mult, ALU.mult))
                    link(v.tensor_tensor(w, w, vv, ALU.mult))
                    link(v.scalar_tensor_tensor(y, w, 1.5, at, ALU.add, ALU.mult))
                    at = y

            def normalize(dst, src, t0, t1):
                for t in range(t0, t1):
                    last = v.bn_stats(bns[0:TOK, t, :], src(t))
                link(last)
                for t in range(t0, t1):
                    last = v.bn_aggr(mv[0:TOK, t, :], bns[0:TOK, t, :])
                link(last)
                rsqrt(mv[0:TOK, t0:t1, 1], t0, t1)
                for t in range(t0, t1):
                    d = dst(t)
                    last = v.tensor_scalar(d, src(t)[:, 0:d.shape[1]], mv[0:TOK, t, 0:1], rs[0:TOK, 0, t:t + 1], ALU.subtract, ALU.mult)
                return last

            def reduce_angle(src, dst):
                link(v.tensor_scalar(dst(0), src, 1 / (2 * math.pi), MAGIC, ALU.mult, ALU.add))
                v.tensor_scalar(dst(1), dst(0), MAGIC, -TWO_PI_A, ALU.subtract, ALU.mult)
                link(v.tensor_scalar(dst(2), dst(0), MAGIC, -TWO_PI_B, ALU.subtract, ALU.mult))
                link(v.tensor_tensor(dst(0), dst(1), src, ALU.add))
                link(v.tensor_tensor(dst(1), dst(0), dst(2), ALU.add))
                v.scalar_tensor_tensor(dst(0), dst(1), -1.0, dst(1), ALU.mult, ALU.max).then_inc(abs_ready, 1)

            dve.wait_ge(gain_in, 16)
            v.memset(gw[:, :, D:D + 1], 1.0)
            for j in range(4):
                dve.wait_ge(w_in[j], 16)
                ks = slice(j * KC, (j + 1) * KC)
                v.tensor_tensor(gw[:, ks, 0:D], wraw[:, ks, :], spread(gcol[:, ks].rearrange("p (k o) -> p k o", o=1), 2, D),
                                ALU.mult).then_inc(gw_ready, 1)
            dve.wait_ge(pool_consts, 1)
            v.tensor_scalar(ident[:, :], diff[:, :], 0.0, None, ALU.is_equal)
            v.tensor_scalar(ident_h[:, :], diff[:, :], 0.0, None, ALU.is_equal)
            v.tensor_scalar(before[:, :], diff[:, :], 0.0, None, ALU.is_lt)
            img = imgd[:, :, :].rearrange("p i r -> p (i r)")
            v.tensor_scalar(mask_f[:, 0, :], img, 0.0, None, ALU.is_equal)
            link(v.tensor_scalar(mask_f[:, 1, :], img, 0.0, BIG, ALU.is_equal, ALU.mult))
            v.scalar_tensor_tensor(mask[:, 0, :], part[:, :], float(IMGS), mask_f[:, 0, :], ALU.is_equal, ALU.add)
            link(v.tensor_scalar(mask_f[:, 2, :], part[:, :], float(IMGS), -BIG, ALU.is_equal, ALU.mult))
            v.tensor_tensor(mask[:, 1, :], mask_f[:, 2, :], mask_f[:, 1, :], ALU.add)
            link(v.tensor_copy(own[:, :], validi[:, 0:1]))
            v.tensor_scalar(slot_iota[:, :], diff[:, :], -1.0, own[:, :], ALU.mult, ALU.add)
            v.tensor_copy(e_iota[:, :], e_iota_i[:, :])
            v.tensor_copy(c_iota[:, :, :], c_iota_i[:, :, :])
            v.tensor_copy(m_iota[:, :, :], m_iota_i[:, :, :])
            v.tensor_scalar(pick_one, part[ONE_Q:TOKX, :], float(TOK - ONE_Q), None, ALU.is_equal)
            v.memset(either[:, TILES, :], 0.0)
            v.memset(topf[:, :, :], 0.0)
            v.memset(top[:, :, :], 0.0)
            v.tensor_scalar(valid[:, :], validi[:, :], float(NTOK), None, ALU.is_lt).then_inc(vec_consts, 1)
            dve.wait_ge(vec_consts, 1)
            dve.wait_ge(bias_in, 16)
            link(v.tensor_tensor(wraw, wraw, spread(bcol[:, :].rearrange("p (k o) -> p k o", o=1), 2, D), ALU.mult))
            v.tensor_reduce(csum, wraw.rearrange("p k d -> p d k"), AX, ALU.add).then_inc(csum_ready, 1)
            dve.wait_ge(consts_in, N_CONSTS)
            reduce_angle(theta_b[0:TOK, :], lambda i: ang[0:TOK, i, 0, :])
            rests(0, NP)
            dve.wait_ge(c_bcast, 1)
            v.tensor_copy(c1[0:TOK, :], pcol(6, 0, D, TOK))
            link(v.tensor_tensor(c2[:, :], pcol(6, D, D), bproj_b[:, :], ALU.add))

            def weighed(g):
                t0, t1 = GROUPS[g]
                n = t1 - t0
                dve.wait_ge(pv_done, t1)
                if g:
                    dve.wait_ge(oT_done, g)
                pv = in_group(g, 0, n * HEADS * DX, TOK).rearrange("p (h d) -> p h d", d=DX)
                rd = rden[0:TOK, 0:n, :].rearrange("p t h -> p (t h)")
                link(v.reciprocal(rd, pv[:, :, DK]))
                v.tensor_tensor(o[0:TOK, 0:n, :].rearrange("p t (h d) -> p (t h) d", d=DK), pv[:, :, 0:DK],
                                spread(rd.rearrange("p (h o) -> p h o", o=1), 2, DK), ALU.mult).then_inc(o_ready, 1)

            def front(g):
                t0, t1 = GROUPS[g]
                n = t1 - t0
                dve.wait_ge(tok_done, t1)
                dve.wait_ge(ssq_done, t1)
                nm, msq, var = (small[0:TOK, i, t0:t1] for i in range(3))
                emb = ps[0:TOK, emb_at(t0):emb_at(t0) + n * 256].rearrange("p (t c) -> p t c", c=256)
                link(v.tensor_scalar(nm, emb[:, :, D], -1.0 / KD, None, ALU.mult))
                link(v.tensor_tensor(msq, nm, nm, ALU.mult))
                link(v.scalar_tensor_tensor(var, ps[0:TOK, ssq_at(t0):ssq_at(t0) + n], 1.0 / KD, msq, ALU.mult, ALU.subtract))
                rsqrt(var, t0, t1)
                for t in range(t0, t1):
                    last = v.scalar_tensor_tensor(y0[0:TOK, t, :], c1[0:TOK, :], small[0:TOK, 0, t:t + 1], emb[:, t - t0, 0:D], ALU.mult, ALU.add)
                link(last)
                for t in range(t0, t1):
                    last = v.scalar_tensor_tensor(y1[0:TOK, t, :], y0[0:TOK, t, :], rs[0:TOK, 0, t:t + 1], c2[0:TOK, :], ALU.mult, ALU.add)
                link(last)
                if g == 2:
                    weighed(0)
                link(normalize(lambda t: y0[0:TOK, t, :], lambda t: y1[0:TOK, t, :], t0, t1))
                row = lambda w: spread(w[0:TOK, :].rearrange("p (o d) -> p o d", o=1), 1, n)
                link(v.tensor_tensor(y1[0:TOK, t0:t1, :], y0[0:TOK, t0:t1, :], row(ln2g_b), ALU.mult))
                link(v.tensor_tensor(h0[0:TOK, t0:t1, :], y1[0:TOK, t0:t1, :], row(ln2b_b), ALU.add))
                link(normalize(lambda t: y0[0:TOK, t, 0:Q], lambda t: h0[0:TOK, t, :], t0, t1))
                dve.wait_ge(cos_ready, g + 1)
                reduce_angle(y0[0:TOK, t0:t1, 0:Q], lambda i: ang[0:TOK, i, 0:n, :])
                dve.wait_ge(cos_ready, g + 2)
                qg = qx[0:TOK, t0:t1, :, 0:DK]
                v.tensor_tensor(qg, ang[0:TOK, 1, 0:n, :].rearrange("p t (h d) -> p t h d", d=DK),
                                spread(ctheta[0:TOK, :].rearrange("p (o h d) -> p o h d", o=1, d=DK), 1, n), ALU.mult).then_inc(q_ready, 1)
                dve.wait_ge(q_ready, g + 1)
                if g:
                    dve.wait_ge(qab_ready, t0)
                link(v.tensor_copy(qh[0:TOK, 0, 0:n, :].rearrange("p t (h d) -> p t h d", d=DK), qg))
                v.tensor_tensor(qh[0:TOK, 1, 0:n, :].rearrange("p t (h d) -> p t h d", d=DK), qg,
                                qh[0:TOK, 0, 0:n, :].rearrange("p t (h d) -> p t h d", d=DK), ALU.subtract).then_inc(qhl_ready, 1)
                dve.wait_ge(qhl_ready, g + 1)
                for t in range(n):
                    for side in range(2):
                        for part_n in range(2):
                            src = spread(qh[0:TOK, part_n, t, :].rearrange("p (h o d) -> p h o d", o=1, d=DK), 2, 2)
                            dst = qab[0:TOK, t0 + t, side]
                            dst = dst[:, :, part_n:4:2, :] if side == 0 else dst[:, :, 2 * part_n:2 * part_n + 2, :]
                            last = v.tensor_copy(dst, src)
                    last.then_inc(qab_ready, 1)

            def normed(g):
                t0, t1 = GROUPS[g]
                n = t1 - t0
                dve.wait_ge(proj_done, g + 1)
                link(v.tensor_tensor(h1[0:TOK, t0:t1, :], h0[0:TOK, t0:t1, :],
                                     in_group(g, 0, n * 256, TOK).rearrange("p (t c) -> p t c", c=256)[:, :, 0:D], ALU.add))
                normalize(lambda t: xs[0:TOK, t, 0, 0:D], lambda t: h1[0:TOK, t, :], t0, t1).then_inc(xn_ready, 1)

            def low_parts(g):
                t0, t1 = GROUPS[g]
                dve.wait_ge(parts_high, g + 1)
                v.tensor_tensor(parts[0:TOK, t0:t1, D:P + P], xs[0:TOK, t0:t1, 0, P:D], parts[0:TOK, t0:t1, P:D], ALU.subtract)
                v.tensor_tensor(parts[0:TOK, t0:t1, P + P:], xs[0:TOK, t0:t1, 0, 0:P], parts[0:TOK, t0:t1, 0:P],
                                ALU.subtract).then_inc(parts_ready, 1)

            def pick(c, step):
                to, second = picks[0:TOK, c % 2], picks[0:TOK, 2]
                slots = spread(slot_iota[0:TOK, :].rearrange("p (o c) -> p o c", o=1), 1, TILES)
                if step < 2:
                    if step == 0 and c >= 2:
                        dve.wait_ge(xcT_done, c - 1)
                    if step == 1 and c >= 1:
                        dve.wait_ge(picks_ready, c)
                    link(v.tensor_tensor(second if step else to, slots, spread(posc[0:TOK, c, step, :].rearrange("p (t o) -> p t o", o=1), 2, CHUNK),
                                         ALU.is_equal))
                else:
                    v.tensor_tensor(to, to, second, ALU.add).then_inc(picks_ready, 1)

            def choose():
                dve.wait_ge(logits_done, len(GROUPS))
                for g, (t0, t1) in enumerate(GROUPS):
                    last = v.tensor_copy(logit[0:TOK, t0:t1, :], in_group(g, LOGITS, (t1 - t0) * E, TOK).rearrange("p (t e) -> p t e", e=E))
                link(last)
                for t in range(TILES):
                    last = v.max(top[0:TOK, t, :], logit[0:TOK, t, :])
                link(last)
                for t in range(TILES):
                    last = v.max_index(topi[0:TOK, t, :], top[0:TOK, t, :], logit[0:TOK, t, :])
                link(last)
                link(v.tensor_copy(topf[0:TOK, :, :], topi[0:TOK, :, :]))

            front(0)
            front(1)
            rests(NP, 14)
            front(2)
            rests(14, 28)
            normed(0)
            rests(28, 33)
            weighed(1)
            rests(33, 37)
            normed(1)
            weighed(2)
            rests(37, 45)
            normed(2)
            low_parts(0)
            low_parts(1)
            rests(45, 52)
            low_parts(2)
            choose()
            v.tensor_tensor(gap[:, :], top[:, :, 1], top[:, :, 0], ALU.subtract).then_inc(gap_ready, 1)
            eb = spread(e_iota[:, :].rearrange("p (o e) -> p o e", o=1), 1, TILES)
            vb = spread(valid[:, :].rearrange("p (t o) -> p t o", o=1), 2, E)
            v.tensor_tensor(hot[:, 0], eb, spread(topf[:, :, 0:1], 2, E), ALU.is_equal)
            link(v.tensor_tensor(hot[:, 1], eb, spread(topf[:, :, 1:2], 2, E), ALU.is_equal))
            link(v.tensor_tensor(posm[:, 0], hot[:, 0], hot[:, 1], ALU.add))
            v.tensor_tensor(either[:, 0:TILES, :], posm[:, 0], vb, ALU.mult).then_inc(either_ready, 1)
            dve.wait_ge(ranks_done, 1)
            te = TILES * E
            link(v.tensor_copy(place[:, :, :].rearrange("p t e -> p (t e)"), pcol(6, 0, te + E)))
            link(v.tensor_tensor(full[:, :, :], spread(place[:, TILES, :].rearrange("p (e o) -> p e o", o=1), 2, TILES), m_iota[:, :, :], ALU.is_gt))
            link(v.tensor_reduce(nch[:, 0, :], full[:, :, :], AX, ALU.add))
            link(v.tensor_tensor_scan(nch[:, 1, :], ones[:, 0:E], nch[:, 0, :], 0.0, ALU.mult, ALU.add))
            ends = nch[:, 1, :]
            link(v.tensor_tensor(base[:, :], ends, nch[:, 0, :], ALU.subtract))
            link(v.scalar_tensor_tensor(place[:, 0:TILES, :], spread(base[:, :].rearrange("p (o e) -> p o e", o=1), 1, TILES),
                                        float(CHUNK), place[:, 0:TILES, :], ALU.mult, ALU.add))
            for k in range(2):
                last = v.tensor_tensor(posm[:, k], hot[:, k], place[:, 0:TILES, :], ALU.mult)
            link(last)
            link(v.tensor_reduce(posf[:, :, :], posm[:, :, :, :], AX, ALU.add))
            v.tensor_copy(posi[:, :, :], posf[:, :, :]).then_inc(pos_ready, 1)
            for c in range(FIRST):
                last = v.tensor_scalar(posc[:, c], posf[:, :, :], 1.0, -float(c * CHUNK), ALU.mult, ALU.add)
            link(last)
            for step in range(3):
                pick(0, step)
            link(v.tensor_tensor(cmp[:, :, :], c_iota[:, :, :], spread(ends.rearrange("p (o e) -> p o e", o=1), 1, CHUNKS), ALU.is_ge))
            link(v.tensor_reduce(cexp[:, :, :].rearrange("p a c -> p (a c)"), cmp[:, :, :], AX, ALU.add))
            link(v.scalar_tensor_tensor(cexp[:, :, :], cexp[:, :, :], float(E - 1), pow8[:, :, :], ALU.min, ALU.mult))
            link(v.tensor_reduce(words[:, :], cexp[:, :, :], AX, ALU.add))
            v.tensor_copy(wordsi[:, :], words[:, :]).then_inc(words_ready, 1)
            rests(52, NP * E)
            for step in range(3):
                pick(1, step)
            dve.wait_ge(gexp_ready, 1)
            link(v.tensor_scalar(wsel[:, 2, :], gexp[:, :], 1.0, None, ALU.add))
            link(v.reciprocal(wsel[:, 0, :], wsel[:, 2, :]))
            link(v.tensor_tensor(wsel[:, 1, :], wsel[:, 0, :], gexp[:, :], ALU.mult))

            def gate(n, s):
                dve.wait_ge(act_ready, n + 1)
                if not (isinstance(n, int) and n < 2):
                    dve.wait_ge(hidT_done, n - 1)
                v.tensor_tensor(hid[:, s % 2, :], act[:, s % 2, :], pcol(s % 3, BLK, BLK), ALU.mult).then_inc(hid_ready, 1)

            def hidden_low(n, s):
                dve.wait_ge(hh_ready, n + 1)
                v.tensor_tensor(hl[:, s % 2], pcol(4 + s % 2, 0, BLK).rearrange("p (h t) -> p h t", h=HT), hh[:, s % 2],
                                ALU.subtract).then_inc(hidT_ready, 1)

            def rows_low(c, j):
                dve.wait_ge(xh_ready, c + 1)
                v.tensor_tensor(x1l[:, j % 2, :], pcol(7, 0, CHUNK), x1h[:, j % 2, 0, :], ALU.subtract)
                v.tensor_tensor(x1h[D2:P, j % 2, 1, :], ps[D2:P, 7 * BANK + CHUNK:7 * BANK + 2 * CHUNK], x1h[D2:P, j % 2, 1, :],
                                ALU.subtract).then_inc(xcT_ready, 1)

            def finish(c, j, reuse):
                dve.wait_ge(down_done, c + 1)
                if reuse:
                    dve.wait_ge(y_out[j % 2], 8 * (c - j) + 16 * (j // 2))
                v.tensor_copy(yc[:, j % 2, :], pcol(Y_BANKS[j % 2], 0, D)).then_inc(y_ready, 1)

            def round4(first, last, c0, n0):
                for s in range(4 * STEPS):
                    j, r = divmod(s, STEPS)
                    gate(n0 + s, s)
                    if not (first and s == 0):
                        hidden_low(n0 + (s - 1), s - 1)
                    if r == 1 and not (last and j == 3) and not (first and j + 1 < FIRST):
                        rows_low(c0 + (j + 1), j + 1)
                    if first and j < FIRST - 2:
                        pick(j + 2, r)
                    if r == 2 and not (first and j == 0):
                        if j == 0:
                            dve.wait_ge(down_done, c0)
                            dve.wait_ge(y_out[1], 8 * c0 - 16)
                            v.tensor_copy(yc[:, 1, :], pcol(Y_BANKS[1], 0, D)).then_inc(y_ready, 1)
                        else:
                            finish(c0 + (j - 1), j - 1, not (first and j - 1 < 2))

            round4(True, False, 0, 0)
            with dve.Fori(1, CHUNKS // 4 - 1) as i:
                round4(False, False, 4 * i, i * (4 * STEPS))
            round4(False, True, CHUNKS - 4, (CHUNKS - 4) * STEPS)
            hidden_low(CHUNKS * STEPS - 1, CHUNKS * STEPS - 1)
            finish(CHUNKS - 1, 3, True)
            dve.wait_ge(got_in[0], 32)
            for t in range(TILES):
                rows = TOK if t < TILES - 1 else LAST
                last = v.scalar_tensor_tensor(h1[0:rows, t, :], got[0:rows, 0, t, :], wsel[0:rows, 0, t:t + 1], h1[0:rows, t, :], ALU.mult, ALU.add)
            link(last)
            dve.wait_ge(got_in[1], 32)
            for t in range(TILES):
                rows = TOK if t < TILES - 1 else LAST
                v.scalar_tensor_tensor(h0[0:rows, t, :], got[0:rows, 1, t, :], wsel[0:rows, 1, t:t + 1], h1[0:rows, t, :], ALU.mult, ALU.add).then_inc(res_ready, 1)

        @block.tensor
        def _(pe):
            mm = nc.tensor.matmul
            tr = nc.tensor.transpose

            def embed(t, k0, k1):
                m = TOKX if t == 0 else TOK
                dst = ps[0:m, emb_at(t):emb_at(t) + D + 1]
                for k in range(k0, k1):
                    if k % KC == 0 and (t == 0 or k == 0):
                        wait_x(pe, t, k // KC)
                        if t == 0:
                            pe.wait_ge(gw_ready, k // KC + 1)
                    last = mm(dst, xbuf[:, t % 2, k, 0:m], gw[:, k, :], start=k == 0, stop=k == KT - 1)
                if k1 == KT:
                    last.then_inc(tok_done, 1)

            def square_sum(t):
                pe.wait_ge(ssq_ready, t + 1)
                for i in range(2):
                    last = mm(ps[0:TOK, ssq_at(t):ssq_at(t) + 1], ssq[:, t % 2, i, :], ones[:, 0:1], start=i == 0, stop=i == 1)
                last.then_inc(ssq_done, 1)

            def turn_queries(t):
                pe.wait_ge(qab_ready, t + 1)
                if t >= 1:
                    pe.wait_ge(qT_ready, t)
                for side in range(2):
                    for a in range(HA):
                        j = side * HA + a
                        src = qab[0:TOK, t, side, a * HB:(a + 1) * HB].rearrange("p h r d -> p (h r d)")
                        last = tr(ps_qT[:, j * TP:j * TP + TOK], src, ident_h[0:TOK, 0:TOK])
                last.then_inc(qT_done, 1)

            def scores(t):
                pe.wait_ge(qT_ready, t + 1)
                for b in range(HB):
                    r = slice(32 * b, 32 * b + 32)
                    dst = ps[0:TOK, (3 + b) * BANK:(3 + b) * BANK + HA * TOK]
                    mm(dst, mask[r, 0, :], spread(mask[r, 1:2, :], 1, HA), start=True, stop=False)
                    for a in range(HA):
                        last = mm(dst[:, a * TOK:(a + 1) * TOK], qabT[r, a, 0:TOK], qabT[r, HA + a, 0:TOK], start=False, stop=a == HA - 1)
                last.then_inc(scores_done, 1)

            def weigh(t):
                pe.wait_ge(probs_ready, t + 1)
                g, i = divmod(t, 2)
                for h in range(HEADS):
                    a, b = divmod(h, HB)
                    c = g * BANK + (i * HEADS + h) * DX
                    last = mm(ps[0:TOK, c:c + DX], probs[0:TOK, b, a, :], qx[0:TOK, t, h, :], start=True, stop=True)
                last.then_inc(pv_done, 1)

            def turn_outputs(g):
                t0, t1 = GROUPS[g]
                pe.wait_ge(o_ready, g + 1)
                for i in range(t1 - t0):
                    last = tr(in_group(g, i * TOK, TOK, Q), o[0:TOK, i, :], ident[0:TOK, 0:TOK])
                last.then_inc(oT_done, 1)

            def project(g):
                t0, t1 = GROUPS[g]
                pe.wait_ge(oT_ready, g + 1)
                for i in range(t1 - t0):
                    last = mm(in_group(g, i * 256, D, TOK), oT[:, i, :], wcomb[:, :], start=True, stop=True)
                last.then_inc(proj_done, 1)

            def turn_normed(g):
                t0, t1 = GROUPS[g]
                pe.wait_ge(xn_ready, g + 1)
                for i in range(t1 - t0):
                    tr(in_group(g, i * TOK, TOK, P), xs[0:TOK, t0 + i, 0, 0:P], ident[0:TOK, 0:TOK])
                    last = tr(in_group(g, (2 + i) * TOK, TOK, D2), xs[0:TOK, t0 + i, 0, P:D], ident[0:TOK, 0:TOK])
                last.then_inc(xnT_done, 1)

            def route(g):
                t0, t1 = GROUPS[g]
                pe.wait_ge(xnT_ready, g + 1)
                for i in range(t1 - t0):
                    mm(in_group(g, LOGITS + i * E, E, TOK), xnT[:, 0, i, :], rt1[:, :], start=True, stop=False)
                    last = mm(in_group(g, LOGITS + i * E, E, TOK), xnT[0:D2, 1, i, :], rt2[:, :], start=False, stop=True)
                last.then_inc(logits_done, 1)

            embed(0, 0, KT)
            embed(1, 0, KT // 2)
            square_sum(0)
            embed(1, KT // 2, KT)
            embed(2, 0, KC)
            square_sum(1)
            embed(2, KC, KT // 2)
            pe.wait_ge(csum_ready, 1)
            mm(pcol(6, D, D), ones[:, :], csum, start=True, stop=True)
            pe.wait_ge(c1_ready, 1)
            mm(pcol(6, 0, D, TOK), pick_one, c1_row, start=True, stop=True).then_inc(c_bcast, 1)
            embed(2, KT // 2, KT)
            square_sum(2)
            embed(3, 0, KT)
            square_sum(3)
            pe.wait_ge(vec_consts, 1)
            pe.wait_ge(consts_in, N_CONSTS)
            turn_queries(0)
            embed(4, 0, 5)
            scores(0)
            turn_queries(1)
            embed(4, 5, 11)
            weigh(0)
            scores(1)
            embed(4, 11, KT)
            square_sum(4)
            weigh(1)
            turn_queries(2)
            scores(2)
            turn_queries(3)
            weigh(2)
            turn_outputs(0)
            scores(3)
            project(0)
            turn_queries(4)
            weigh(3)
            scores(4)
            turn_outputs(1)
            project(1)
            weigh(4)
            turn_normed(0)
            turn_outputs(2)
            turn_normed(1)
            project(2)
            route(0)
            route(1)
            turn_normed(2)
            route(2)

            pe.wait_ge(either_ready, 1)
            mm(pcol(6, 0, (TILES + 1) * E), before[:, :], either[:, :, :].rearrange("p t e -> p (t e)"), start=True, stop=False)
            for t in range(TILES):
                last = mm(pcol(6, (t + 1) * E, (TILES - t) * E), ones_b[:, :], spread(either[:, t:t + 1, :], 1, TILES - t),
                          start=False, stop=t == TILES - 1)
            last.then_inc(ranks_done, 1)

            def pick_rows(c):
                pe.wait_ge(picks_ready, c + 1)
                pe.wait_ge(parts_ready, len(GROUPS))
                if c:
                    pe.wait_ge(xcT_ready, c)
                for part_n in range(3):
                    for t in range(TILES):
                        rows = TOK if t < TILES - 1 else LAST
                        last = mm(pcol(7, part_n * CHUNK, CHUNK), parts[0:rows, t, part_n * P:(part_n + 1) * P], picks[0:rows, c % 2, t, :],
                                  start=t == 0, stop=t == TILES - 1)
                last.then_inc(xcT_done, 1)

            def turn_rows(c, j):
                if isinstance(c, int) and c < FIRST:
                    return pick_rows(c)
                pe.wait_ge(xc_in[j % 4], 4 * (c - j % 4) + 16)
                pe.wait_ge(xcT_ready, c)
                tr(pcol(7, 0, CHUNK), xc[:, j % 4, 0:P], ident[:, :])
                tr(pcol(7, CHUNK, CHUNK), xc[:, j % 4, P:P + CHUNK], ident[:, :]).then_inc(xcT_done, 1)

            turn_rows(0, 0)
            pe.wait_ge(words_ready, 1)
            word = [pe.alloc_register(f"chunk_word{k}") for k in range(2)]
            offs = [pe.alloc_register(f"expert_off{k}") for k in range(2)]
            TOP = 8 ** (CHUNKS // 2) - 1
            for k in range(2):
                pe.reg_mov(word[k], pe.value_load(wordsi[0:1, k:k + 1], min_val=0, max_val=TOP))

            def part_w(which, off, col, n):
                return (hi_w if which == 0 else lo_w)[:, bass.ds(off + (which * EW + col), n)]

            def gate_up(n, s, off):
                if not (isinstance(n, int) and n < 3):
                    pe.wait_ge(hid_ready, n - 2)
                j, r = divmod(s, STEPS)
                dst = pcol(s % 3, 0, 2 * BLK)
                k1, k2 = 2 * BLK * r, W2 + 2 * BLK * r
                mm(dst, x1h[:, j % 2, 0, :], part_w(0, off, k1, 2 * BLK), start=True, stop=False)
                mm(dst, x1h[:, j % 2, 0, :], part_w(1, off, k1, 2 * BLK), start=False, stop=False)
                mm(dst, x1l[:, j % 2, :], part_w(0, off, k1, 2 * BLK), start=False, stop=False)
                mm(dst, x1h[:, j % 2, 1, :], part_w(0, off, k2, 2 * BLK), start=False, stop=False)
                mm(dst, x1h[:, j % 2, 1, :], part_w(1, off, k2, 2 * BLK), start=False, stop=True).then_inc(gu_done, 1)

            def turn_hidden(n, s):
                pe.wait_ge(hid_ready, n + 1)
                if not (isinstance(n, int) and n < 2):
                    pe.wait_ge(hidT_ready, n - 1)
                for h in range(HT):
                    last = tr(pcol(4 + s % 2, h * P, P), hid[:, s % 2, h * P:(h + 1) * P], ident[:, :])
                last.then_inc(hidT_done, 1)

            def down(c, n, s, off):
                y = pcol(Y_BANKS[s // STEPS % 2], 0, D)
                pe.wait_ge(hidT_ready, n + 1)
                r = s % STEPS
                if r == 0 and not (isinstance(c, int) and c < 2):
                    pe.wait_ge(y_ready, c - 1)
                for h in range(HT):
                    k = r * HT + h
                    col = 2 * W2 + k * D
                    end = k == STEPS * HT - 1
                    mm(y, hh[:, s % 2, h, :], part_w(0, off, col, D), start=k == 0, stop=False)
                    mm(y, hh[:, s % 2, h, :], part_w(1, off, col, D), start=False, stop=False)
                    last = mm(y, hl[:, s % 2, h, :], part_w(0, off, col, D), start=False, stop=end)
                if r == STEPS - 1:
                    last.then_inc(down_done, 1)

            def offset(k):
                return pe.snap(offs[k], min_val=0, max_val=(E - 1) * 2 * EW)

            def round4(first, last, c0, n0):
                for s in range(4 * STEPS):
                    j, r = divmod(s, STEPS)
                    if r == 0:
                        w0 = pe.snap(word[0], min_val=0, max_val=TOP)
                        pe.reg_mov(offs[j % 2], ((w0 >> (3 * j)) & 7) * (2 * EW))
                    off = offset(j % 2)
                    if r == 0:
                        pe.wait_ge(xcT_ready, c0 + (j + 1))
                    if first and s == 0:
                        for n in (NP * E - 1, NP * E - 2):
                            pe.wait_ge(split_pool if on_pool(n) else split_vec, splits(n))
                    gate_up(n0 + s, s, off)
                    if not (first and s < 1):
                        turn_hidden(n0 + (s - 1), s - 1)
                    if r == 1 and not (last and j == 3):
                        turn_rows(c0 + (j + 1), j + 1)
                    if not (first and s < 2):
                        jd = (s - 2) // STEPS
                        down(c0 + jd, n0 + (s - 2), s - 2, offset(jd % 2))
                w0 = pe.snap(word[0], min_val=0, max_val=TOP)
                w1 = pe.snap(word[1], min_val=0, max_val=TOP)
                pe.reg_mov(word[0], (w0 >> 12) | ((w1 & 4095) << 12))
                pe.reg_mov(word[1], w1 >> 12)

            round4(True, False, 0, 0)
            with pe.Fori(1, CHUNKS // 4 - 1) as i:
                round4(False, False, 4 * i, i * (4 * STEPS))
            round4(False, True, CHUNKS - 4, (CHUNKS - 4) * STEPS)
            S = CHUNKS * STEPS
            down(CHUNKS - 1, S - 2, S - 2, offset(1))
            turn_hidden(S - 1, S - 1)
            down(CHUNKS - 1, S - 1, S - 1, offset(1))


def kernel(x, L0_tok_ln1_g, L0_tok_ln1_b, L0_tok_W_proj, L0_tok_b_proj, L0_tok_ln2_g, L0_tok_ln2_b,
           L0_attn_theta, L0_attn_W_combine, L0_ffn_router_w, L0_ffn_Wg, L0_ffn_Wu, L0_ffn_Wd):
    import numpy as np
    import concourse.bacc as bacc
    from concourse.bass_utils import run_bass_kernel_spmd

    P, PATCH, SEQ, IMGS, TILES, BLK = 128, 32, 9, 13, 5, 256
    x = np.asarray(x)
    B, C, H, W = x.shape
    tok = x.reshape(B, C, H // PATCH, PATCH, W // PATCH, PATCH).transpose(0, 2, 4, 3, 5, 1).reshape(B * SEQ, -1)
    K = tok.shape[1]
    KT = K // P
    TOK = IMGS * SEQ
    full = np.zeros((TILES * TOK, K), tok.dtype)
    full[:B * SEQ] = tok
    full = np.concatenate([full.reshape(TILES, TOK, K), np.ones((TILES, 1, K), tok.dtype)], axis=1)
    xt = full.reshape(TILES, TOK + 1, P, KT).transpose(0, 2, 3, 1)
    Wg, Wu, Wd = (np.asarray(a) for a in (L0_ffn_Wg, L0_ffn_Wu, L0_ffn_Wd))
    E, HID, D = Wg.shape
    gu = np.stack([Wg.transpose(0, 2, 1).reshape(E, D, HID // BLK, BLK),
                   Wu.transpose(0, 2, 1).reshape(E, D, HID // BLK, BLK)], axis=3).reshape(E, D, 2 * HID)
    wd = Wd.transpose(0, 2, 1).reshape(E, HID // P, P, D).transpose(0, 2, 1, 3).reshape(E, P, -1)
    w_exp = np.concatenate([gu[:, :P], np.concatenate([gu[:, P:], gu[:, P:]], axis=1), wd], axis=2)
    ins = {
        "x_t": xt,
        "ln1_g": np.asarray(L0_tok_ln1_g).reshape(P, KT), "ln1_b": np.asarray(L0_tok_ln1_b).reshape(P, KT),
        "w_proj": np.asarray(L0_tok_W_proj), "b_proj": np.asarray(L0_tok_b_proj),
        "ln2_g": np.asarray(L0_tok_ln2_g), "ln2_b": np.asarray(L0_tok_ln2_b),
        "theta": np.asarray(L0_attn_theta), "w_comb": np.asarray(L0_attn_W_combine).T,
        "router": np.asarray(L0_ffn_router_w).T, "w_exp": w_exp,
    }
    ins = {k: np.ascontiguousarray(a) for k, a in ins.items()}
    nc = bacc.Bacc("TRN2", target_bir_lowering=False, num_devices=1)
    args = [nc.dram_tensor(k, a.shape, mybir.dt.from_np(a.dtype), kind="ExternalInput").ap() for k, a in ins.items()]
    n_tok = B * SEQ
    chunks = (2 * n_tok + E * (P - 1)) // P
    args.append(nc.dram_tensor("out", (n_tok, D), mybir.dt.float32, kind="ExternalOutput").ap())
    args.append(nc.dram_tensor("slot_x", (chunks * P, 2 * P + 1), mybir.dt.float32, kind="Internal").ap())
    args.append(nc.dram_tensor("pair_y", (2 * n_tok + chunks * P, D), mybir.dt.float32, kind="Internal").ap())
    vit_tower(nc, *args)
    r = run_bass_kernel_spmd(nc, [ins], core_ids=[0])
    return r.results[0]["out"].reshape(B, SEQ, D)
```
